# Optimizing a Trainium2 kernel written in Bass

```python
import numpy as np
import jax
import jax.numpy as jnp

def _softmax(x, axis=-1):
    return jax.nn.softmax(x, axis=axis)

def _gelu(x):
    return jax.nn.gelu(x, approximate=True)

def _silu(x):
    return jax.nn.silu(x)

def _sigmoid(x):
    return jax.nn.sigmoid(x)

def _layernorm(x, axis=-1, eps=1e-05):
    m = jnp.mean(x, axis=axis, keepdims=True)
    v = jnp.var(x, axis=axis, keepdims=True)
    return (x - m) / jnp.sqrt(v + eps)

def _scatter_add(tgt, idx, src, axis=0):
    return tgt.at[idx].add(src)

def _segment_sum(src, seg, n):
    return jax.ops.segment_sum(src, seg, n)
kernel_name = 'mk_adaln_d1_jaxref_r8_02bd31'

def setup_inputs(seed: int=0):
    np.random.seed(seed)
    _w = jnp.asarray

    def _L0_attn_setup():
        import jax, jax.numpy as jnp
        import numpy as np
        B, T, D, H = (2, 256, 128, 4)
        DK, DV = (128, 256)
        HK, HV = (DK // H, DV // H)
        LR = 16
        EPS = 1e-05
        GATE_NORM = 16.0

        def _xavier(k, shape, gain):
            fan_in, fan_out = shape
            lim = gain * np.sqrt(6.0 / (fan_in + fan_out))
            return jax.random.uniform(k, shape, jnp.float32, -lim, lim)

        def _gla_scan(q, k, v, g):
            S0 = jnp.zeros((q.shape[-1], v.shape[-1]), q.dtype)

            def step(S, inp):
                qt, kt, vt, gt = inp
                S = jnp.exp(gt)[:, None] * S + kt[:, None] * vt[None, :]
                return (S, qt @ S)
            return jax.lax.scan(step, S0, (q, k, v, g))[1]

        def _forward(x, Wq, Wk, Wv, Wg, gk_w1, gk_w2, gk_b, Wo, rms_w):
            b, t = (x.shape[0], x.shape[1])
            scale = HK ** (-0.5)
            q = (x @ Wq).reshape(b, t, H, HK).transpose(0, 2, 1, 3) * scale
            k = (x @ Wk).reshape(b, t, H, HK).transpose(0, 2, 1, 3)
            v = (x @ Wv).reshape(b, t, H, HV).transpose(0, 2, 1, 3)
            gl = x @ gk_w1 @ gk_w2 + gk_b
            g = jax.nn.log_sigmoid(gl.astype(jnp.float32)) / GATE_NORM
            g = g.reshape(b, t, H, HK).transpose(0, 2, 1, 3)
            o = jax.vmap(jax.vmap(_gla_scan))(q, k, v, g)
            o = o.transpose(0, 2, 1, 3)
            o = o * jax.lax.rsqrt(jnp.mean(o * o, axis=-1, keepdims=True) + EPS) * rms_w
            o = o.reshape(b, t, DV) * jax.nn.silu(x @ Wg)
            return o @ Wo
        key = jax.random.key(seed)
        ks = jax.random.split(key, 10)
        g_qkv = 2 ** (-2.5)
        return {'x': jax.random.normal(ks[0], (B, T, D), jnp.float32), 'Wq': _xavier(ks[1], (D, DK), g_qkv), 'Wk': _xavier(ks[2], (D, DK), g_qkv), 'Wv': _xavier(ks[3], (D, DV), g_qkv), 'Wg': _xavier(ks[4], (D, DV), g_qkv), 'gk_w1': _xavier(ks[5], (D, LR), g_qkv), 'gk_w2': _xavier(ks[6], (LR, DK), g_qkv), 'gk_b': jnp.zeros((DK,), jnp.float32), 'Wo': _xavier(ks[7], (DV, D), 2 ** (-1)), 'rms_w': jnp.ones((HV,), jnp.float32)}
    _L0_attn_in = _L0_attn_setup()

    def _L0_ffn_setup():
        import jax, jax.numpy as jnp
        import numpy as np
        B, S, D, E, K = (4, 256, 128, 8, 2)
        H = 4 * D
        key = jax.random.key(seed)
        k0, k1, k2, k3 = jax.random.split(key, 4)
        x = jax.random.normal(k0, (B, S, D), dtype=jnp.float32)
        router_w = jax.random.normal(k1, (E, D), dtype=jnp.float32) * 0.02
        w1 = jax.random.normal(k2, (E, H, D), dtype=jnp.float32) * 0.02
        w2 = jax.random.normal(k3, (E, D, H), dtype=jnp.float32) * 0.02
        return {'x': x, 'router_w': router_w, 'w1': w1, 'w2': w2}
    _L0_ffn_in = _L0_ffn_setup()
    _L0_c = _w((lambda *s: np.random.randn(*s).astype(np.float32) * 0.05)(8, 128))
    _L0_wmod = _w((lambda *s: np.random.randn(*s).astype(np.float32) * 0.05)(128, 6 * 128) * 128 ** (-0.5))
    _d = {'L0_attn_x': _L0_attn_in['x'], 'L0_attn_Wq': _L0_attn_in['Wq'], 'L0_attn_Wk': _L0_attn_in['Wk'], 'L0_attn_Wv': _L0_attn_in['Wv'], 'L0_attn_Wg': _L0_attn_in['Wg'], 'L0_attn_gk_w1': _L0_attn_in['gk_w1'], 'L0_attn_gk_w2': _L0_attn_in['gk_w2'], 'L0_attn_gk_b': _L0_attn_in['gk_b'], 'L0_attn_Wo': _L0_attn_in['Wo'], 'L0_attn_rms_w': _L0_attn_in['rms_w'], 'L0_ffn_router_w': _L0_ffn_in['router_w'], 'L0_ffn_w1': _L0_ffn_in['w1'], 'L0_ffn_w2': _L0_ffn_in['w2'], 'L0_c': _L0_c, 'L0_wmod': _L0_wmod}
    _x0 = _d['L0_attn_x']
    _d['L0_attn_x'] = jax.random.normal(jax.random.fold_in(jax.random.key(seed), 1), (8, 512, 128), dtype=_x0.dtype)
    del _x0
    return _d

def reference(L0_attn_x, L0_attn_Wq, L0_attn_Wk, L0_attn_Wv, L0_attn_Wg, L0_attn_gk_w1, L0_attn_gk_w2, L0_attn_gk_b, L0_attn_Wo, L0_attn_rms_w, L0_ffn_router_w, L0_ffn_w1, L0_ffn_w2, L0_c, L0_wmod):

    def _L0_attn_ref(x, Wq, Wk, Wv, Wg, gk_w1, gk_w2, gk_b, Wo, rms_w):
        import jax, jax.numpy as jnp
        import numpy as np
        B, T, D, H = (2, 256, 128, 4)
        DK, DV = (128, 256)
        HK, HV = (DK // H, DV // H)
        LR = 16
        EPS = 1e-05
        GATE_NORM = 16.0

        def _xavier(k, shape, gain):
            fan_in, fan_out = shape
            lim = gain * np.sqrt(6.0 / (fan_in + fan_out))
            return jax.random.uniform(k, shape, jnp.float32, -lim, lim)

        def _gla_scan(q, k, v, g):
            S0 = jnp.zeros((q.shape[-1], v.shape[-1]), q.dtype)

            def step(S, inp):
                qt, kt, vt, gt = inp
                S = jnp.exp(gt)[:, None] * S + kt[:, None] * vt[None, :]
                return (S, qt @ S)
            return jax.lax.scan(step, S0, (q, k, v, g))[1]

        def _forward(x, Wq, Wk, Wv, Wg, gk_w1, gk_w2, gk_b, Wo, rms_w):
            b, t = (x.shape[0], x.shape[1])
            scale = HK ** (-0.5)
            q = (x @ Wq).reshape(b, t, H, HK).transpose(0, 2, 1, 3) * scale
            k = (x @ Wk).reshape(b, t, H, HK).transpose(0, 2, 1, 3)
            v = (x @ Wv).reshape(b, t, H, HV).transpose(0, 2, 1, 3)
            gl = x @ gk_w1 @ gk_w2 + gk_b
            g = jax.nn.log_sigmoid(gl.astype(jnp.float32)) / GATE_NORM
            g = g.reshape(b, t, H, HK).transpose(0, 2, 1, 3)
            o = jax.vmap(jax.vmap(_gla_scan))(q, k, v, g)
            o = o.transpose(0, 2, 1, 3)
            o = o * jax.lax.rsqrt(jnp.mean(o * o, axis=-1, keepdims=True) + EPS) * rms_w
            o = o.reshape(b, t, DV) * jax.nn.silu(x @ Wg)
            return o @ Wo
        return _forward(x, Wq, Wk, Wv, Wg, gk_w1, gk_w2, gk_b, Wo, rms_w)

    def _L0_ffn_ref(x, router_w, w1, w2):
        import jax, jax.numpy as jnp
        import numpy as np
        B, S, D, E, K = (4, 256, 128, 8, 2)
        H = 4 * D
        b, s, d = x.shape
        e = router_w.shape[0]
        logits = jnp.einsum('bsd,ed->bse', x, router_w)
        probs = jax.nn.softmax(logits, axis=-1)
        topk_vals, topk_idx = jax.lax.top_k(probs, K)
        x_flat = x.reshape(b * s, d)
        vals = topk_vals.reshape(b * s, K)
        idx = topk_idx.reshape(b * s, K)
        out = jnp.zeros_like(x_flat)
        for eid in range(e):
            w = jnp.sum(jnp.where(idx == eid, vals, jnp.zeros((), x.dtype)), axis=-1)
            h = jax.nn.gelu(x_flat @ w1[eid].T, approximate=False)
            y = h @ w2[eid].T
            out = out + w[:, None] * y
        return out.reshape(b, s, d)
    x = L0_attn_x
    mod = (_silu(L0_c) @ L0_wmod).reshape(L0_c.shape[0], 6, 1, -1)
    sa, ca, ga, sb, cb, gb = (mod[:, 0], mod[:, 1], mod[:, 2], mod[:, 3], mod[:, 4], mod[:, 5])
    ga = (2 * (ga >= 0) - 1) * jnp.maximum(jnp.abs(ga), 0.25)
    gb = (2 * (gb >= 0) - 1) * jnp.maximum(jnp.abs(gb), 0.25)
    h = _layernorm(x, axis=-1) * (1 + ca) + sa
    x = x + ga * _L0_attn_ref(h, L0_attn_Wq, L0_attn_Wk, L0_attn_Wv, L0_attn_Wg, L0_attn_gk_w1, L0_attn_gk_w2, L0_attn_gk_b, L0_attn_Wo, L0_attn_rms_w)
    h = _layernorm(x, axis=-1) * (1 + cb) + sb
    x = x + gb * _L0_ffn_ref(h, L0_ffn_router_w, L0_ffn_w1, L0_ffn_w2)
    return x

_drawn_inputs = setup_inputs


def setup_inputs(seed=0):
    import zlib

    import numpy as np

    out = dict(_drawn_inputs(seed))
    spreads = {'L0_attn_gk_b': (0.0, 0.8), 'L0_attn_rms_w': (1.0, 0.6)}
    factors = {'L0_attn_Wq': 5.2,
     'L0_attn_Wk': 5.155,
     'L0_attn_Wv': 5.154,
     'L0_attn_Wg': 5.241,
     'L0_attn_gk_w1': 8.0,
     'L0_attn_gk_w2': 8.0,
     'L0_attn_Wo': 5.177,
     'L0_ffn_router_w': 8.0,
     'L0_ffn_w1': 8.0,
     'L0_ffn_w2': 8.0,
     'L0_c': 5.06,
     'L0_wmod': 4.969}
    for name, (base, spread) in spreads.items():
        noise = np.random.default_rng([zlib.crc32(name.encode()), seed]).standard_normal(out[name].shape)
        drawn = base * np.exp(spread * noise) if base else spread * noise
        out[name] = jnp.asarray(drawn.astype(out[name].dtype))
    for name, factor in factors.items():
        out[name] = (out[name] * factor).astype(out[name].dtype)
    return out
```

```python
from contextlib import ExitStack

import numpy as np

import concourse.bass as bass
from concourse import mybir

F32 = mybir.dt.float32
ALU = mybir.AluOpType
ACT = mybir.ActivationFunctionType
AX = mybir.AxisListType

P = 128
B, T, D = 8, 512, 128
H, HK, HV = 4, 32, 64
DK, DV = H * HK, H * HV
LR = 16
C = T // P
SUB = 32
NS = P // SUB
E, HID = 8, 512
KH = HID // P
EPS = 1e-5
GATE_NORM = 16.0
MODS = 6


def build_program(nc, x, cT, wmod, wq, wk, wvg, gk_w1, gk_w2, gk_b, wo, rms_w, rwT, w1T, w2T, out):
    with ExitStack() as ctx:
        def sb(name, shape, dt=F32):
            return ctx.enter_context(nc.sbuf_tensor(name, shape, dt))

        def bank(name):
            return ctx.enter_context(nc.psum_tensor(name, [P, 512], F32))

        def sem(name):
            return ctx.enter_context(nc.semaphore(name))

        X = sb("X", [P, B, C, D])
        X2 = X
        H2T = sb("H2T", [P, B, T])
        WGT = sb("WGT", [P, B, C, E])
        Wmod = sb("Wmod", [P, MODS * D])
        CT = sb("CT", [P, B])
        Wq, Wk = sb("Wq", [P, DK]), sb("Wk", [P, DK])
        Wvg = sb("Wvg", [P, 2 * DV])
        W1k, W2k = sb("W1k", [P, LR]), sb("W2k", [LR, DK])
        Gb = sb("Gb", [P, 1])
        WoR, Wo = sb("WoR", [P, 2, D]), sb("Wo", [P, 2, D])
        RmsW = sb("RmsW", [P, 1])
        Rw = sb("Rw", [P, E])
        Big = sb("Big", [P, 2, 2, C * NS * P])
        W1 = Big[:, 0, :, :].rearrange("p a n -> p (a n)").rearrange("p (e n) -> p e n", e=E)
        W2 = Big[:, 1, :, :].rearrange("p a n -> p (a n)").rearrange("p (e k d) -> p e k d", e=E, k=KH)
        Id = sb("Id", [P, P])
        Causal = sb("Causal", [P, P])
        HeadMask = sb("HeadMask", [P, H, HV])
        Restart = sb("Restart", [P, C, P])
        Before = sb("Before", [P, E, E])
        EpsC = sb("EpsC", [P, 1])
        SC = sb("SC", [P, 4, B])
        SilC = sb("SilC", [P, B])
        Cols = sb("Cols", [P, 2, B])
        Rows = sb("Rows", [P, B, 4, D])
        Sgn = H2T[:].rearrange("p b (j d) -> p b j d", j=4)
        St6 = sb("St6", [P, 2, C, 6])
        Pad = sb("Pad", [P, 1])
        MV = sb("MV", [P, 2, C, 2])
        LnV, Rstd = sb("LnV", [P, 2, C]), sb("Rstd", [P, 2, C])
        Xh = sb("Xh", [P, C, D])
        HT = sb("HT", [P, T])
        UT = sb("UT", [LR, T])
        Q, K = sb("Q", [P, T]), sb("K", [P, C, P])
        GL, Ln1 = sb("GL", [P, T]), sb("Ln1", [P, T])
        G16 = sb("G16", [P, T])
        Cum = sb("Cum", [P, C, NS, SUB])
        decayed = [Big[:, i // 2, i % 2, :].rearrange("p (c i s) -> p c i s", c=C, i=NS) for i in range(4)]
        DifK, ExpK, KT = decayed[0], decayed[1], decayed[2:4]
        DifQ = sb("DifQ", [P, 2, T])
        ExpQ = sb("ExpQ", [P, 2, T])
        ExpB = [sb(f"ExpB{u}", [P, T]) for u in range(2)]
        KE = [sb(f"KE{u}", [P, C, P]) for u in range(2)]
        QB = [sb(f"QB{u}", [P, H, T]) for u in range(2)]
        QE = sb("QE", [P, T])
        QS = [sb(f"QS{u}", [P, T]) for u in range(2)]
        VG = [sb(f"VG{u}", [P, C, 2 * DV]) for u in range(2)]
        AbsG = sb("AbsG", [P, C, DV])
        Gate = [VG[u][:, :, DV:] for u in range(2)]
        KEt = sb("KEt", [P, 3, P])
        PT = [sb(f"PT{i}", [P, H, P]) for i in range(2)]
        S = [sb(f"S{c}", [P, DV]) for c in range(3)]
        Stmp = sb("Stmp", [P, 2, DV])
        O = sb("O", [P, C, DV])
        SilB = O[:].rearrange("p c v -> p (c v)").rearrange("p (b n) -> p b n", b=B)
        Sq = sb("Sq", [P, C, DV])
        Ms = sb("Ms", [P, 2, C * H])
        OT = sb("OT", [P, 2, T])
        At = sb("At", [P, C, D])
        H2 = sb("H2", [P, C, D])
        H2Tb = sb("H2Tb", [P, T])
        LG = sb("LG", [P, C, E])
        Rk = sb("Rk", [P, 3, C, E, E])
        Sm = sb("Sm", [P, 4, C, E])
        R1 = sb("R1", [P, 4, C])
        GH, Acc, Yo = QB, H2, At

        psA = [bank(f"ps{i}") for i in range(8)]
        psT, pjA, pjB, psS0, psS1, psK, psD, psO = psA

        names = ("x_in0 x_in1 x_in2 c_in wmod_in proj_in attn_in ffn_in ident_a ident const zeroed silu_abs silu_exp silu_ln "
                 "silu_min silu_sig silu_c silu_b cols_ps cols rows_ps rows rows_used rows_abs rows_sgn rows_mul rows_fin wo_fin "
                 "bn1 mv1 lnv1 rstd1 xhat1 xT1 hT uT_ps uT q_ps q_sb gl_ps gl_sb k_ps k_sb vg_ps vgA vgB abs1 ex1 ln1 "
                 "g16 cum difk difq expk expq expb ktil qe hmask qblk qs kend absg exg lng ming sigg gate "
                 "ket_ps ket sc_ps pt ds_ps s_tmp s_st o_ps o_sb sq ms lnms rms onrm ogat oT_psa oT_psb oTa oTb "
                 "at_ps at_g x2 bn2 mv2 lnv2 rstd2 xhat2 h2m h2 xT2 h2T h2T_all lg_ps lg "
                 "rk0 rk1 rk2 rk3 rk4 mx sh ex sum rsum pr wgt h_ps gelu y_ps acc y_gb y_fin out_dma").split()
        s = {n: sem(n) for n in names}

        def wait(eng, name, value):
            if isinstance(value, int) and value <= 0:
                return
            eng.wait_ge(s[name], value)

        block = ctx.enter_context(nc.Block())

        def pipeline(eng, stage1, stage2, stage3):
            stage1(0, 0)
            stage1(1, 1)
            stage2(0, 0)
            with eng.Fori(0, (B - 2) // 2) as i:
                for u, b in ((1, i * 2 + 1), (0, i * 2 + 2)):
                    stage1(b + 1, 1 - u)
                    stage3(b - 1)
                    stage2(b, u)
            stage3(B - 2)
            stage2(B - 1, 1)
            stage3(B - 1)

        @block.sync
        def _(sp):
            sp.dma_start(CT[:], cT).then_inc(s["c_in"], 16)
            sp.dma_start(Wmod[:], wmod).then_inc(s["wmod_in"], 16)
            xv = x.rearrange("b (c p) d -> p b c d", p=P)
            for b, end in ((0, 1), (1, 2), (2, B)):
                sp.dma_start(X[:, b:end, :, :], xv[:, b:end, :, :]).then_inc(s[f"x_in{b}"], 16)
                if b == 0:
                    for dst, src in ((Wq, wq), (Wk, wk), (Wvg, wvg), (W1k, gk_w1), (W2k, gk_w2), (Gb, gk_b)):
                        sp.dma_start(dst[:], src).then_inc(s["proj_in"], 16)
                    sp.dma_start(WoR[:], wo).then_inc(s["attn_in"], 16)
                    sp.dma_start(Rw[:], rwT).then_inc(s["attn_in"], 16)
                    for j in range(2):
                        sp.dma_start(RmsW[j * HV:(j + 1) * HV, :], rms_w).then_inc(s["attn_in"], 16)
            sp.wait_ge(s["sc_ps"], B * C)
            sp.wait_ge(s["ktil"], B)
            sp.dma_start(W1, w1T).then_inc(s["ffn_in"], 16)
            sp.dma_start(W2, w2T).then_inc(s["ffn_in"], 16)
            ov = out.rearrange("b (c p) d -> p b c d", p=P)
            with sp.Fori(0, B) as n:
                sp.wait_ge(s["y_fin"], n + 1)
                sp.dma_start(ov[:, n, :, :], Yo[:]).then_inc(s["out_dma"], 16)
            sp.wait_ge(s["out_dma"], 16 * B)

        @block.gpsimd
        def _(pool):
            nc.gpsimd.memset(Id[:], 0.0).then_inc(s["ident_a"], 1)
            nc.gpsimd.memset(Causal[:], 1.0).then_inc(s["ident_a"], 1)
            nc.gpsimd.memset(Restart[:], 1.0).then_inc(s["ident_a"], 1)
            nc.gpsimd.memset(Before[:], 1.0).then_inc(s["ident_a"], 1)
            nc.gpsimd.memset(EpsC[:], EPS).then_inc(s["const"], 1)
            pool.wait_ge(s["ident_a"], 4)
            nc.gpsimd.affine_select(out=Id[:], in_=Id[:], compare_op=ALU.not_equal, fill=1.0, base=0,
                                    pattern=[[-1, P]], channel_multiplier=1).then_inc(s["ident"], 1)
            nc.gpsimd.affine_select(out=Causal[:], in_=Causal[:], compare_op=ALU.is_ge, fill=0.0, base=0,
                                    pattern=[[1, P]], channel_multiplier=-1).then_inc(s["const"], 1)
            nc.gpsimd.memset(Restart[:, :, 0:1], 0.0).then_inc(s["const"], 1)
            nc.gpsimd.affine_select(out=Before[:], in_=Before[:], compare_op=ALU.is_gt, fill=0.0, base=0,
                                    pattern=[[1, E], [-1, E]], channel_multiplier=0).then_inc(s["const"], 1)
            nc.gpsimd.memset(DifK, 0.0).then_inc(s["zeroed"], 1)

            def stage1(b, u):
                wait(pool, "expq", b + 1)
                wait(pool, "q_sb", b + 1)
                wait(pool, "qblk", H * b)
                nc.gpsimd.tensor_tensor(QE[:], Q[:], ExpQ[:, 0, :], ALU.mult).then_inc(s["qe"], 1)
                wait(pool, "expb", b + 1)
                nc.gpsimd.tensor_tensor(QS[u][:], Q[:], ExpB[u][:], ALU.mult).then_inc(s["qs"], 1)
                wait(pool, "sigg", b + 1)
                nc.gpsimd.tensor_tensor(Gate[u], VG[u][:, :, DV:], AbsG[:], ALU.mult).then_inc(s["gate"], 1)

            def stage2(b, u):
                wait(pool, "at_g", b + 1)
                nc.gpsimd.tensor_tensor(X2[:, b, :, :], X[:, b, :, :], At[:], ALU.add).then_inc(s["x2"], 1)

            def stage3(b):
                wait(pool, "xhat2", C * b + C)
                wait(pool, "rows_fin", 1)
                wait(pool, "xT2", b)
                nc.gpsimd.tensor_tensor(H2[:], H2[:], Rows[:, b, 2:3, :].to_broadcast([P, C, D]), ALU.mult).then_inc(s["h2m"], 1)
                wait(pool, "h2m", b + 1)
                nc.gpsimd.tensor_tensor(H2[:], H2[:], Rows[:, b, 1:2, :].to_broadcast([P, C, D]), ALU.add).then_inc(s["h2"], 1)

            pipeline(pool, stage1, stage2, stage3)

        @block.scalar
        def _(act):
            act.wait_ge(s["c_in"], 16)
            nc.scalar.activation(SC[:, 0, :], CT[:], ACT.Abs).then_inc(s["silu_abs"], 1)
            act.wait_ge(s["silu_abs"], 1)
            nc.scalar.activation(SC[:, 1, :], SC[:, 0, :], ACT.Exp, scale=-1.0).then_inc(s["silu_exp"], 1)
            act.wait_ge(s["silu_exp"], 1)
            nc.scalar.activation(SC[:, 2, :], SC[:, 1, :], ACT.Ln, bias=1.0).then_inc(s["silu_ln"], 1)
            act.wait_ge(s["silu_min"], 1)
            nc.scalar.activation(SC[:, 3, :], SC[:, 3, :], ACT.Exp).then_inc(s["silu_sig"], 1)
            act.wait_ge(s["cols_ps"], 1)
            nc.scalar.activation(Cols[:, 0, :], psT[:, 0:B], ACT.Copy).then_inc(s["cols"], 1)
            nc.scalar.activation(Cols[:, 1, :], psT[:, B:2 * B], ACT.Identity, bias=1.0).then_inc(s["cols"], 1)

            def rstd(b, k, mv, lnv, out):
                wait(act, mv, C * b + C)
                nc.scalar.activation(LnV[:, k, :], MV[:, k, :, 1], ACT.Ln, bias=EpsC[:]).then_inc(s[lnv], 1)
                wait(act, lnv, b + 1)
                nc.scalar.activation(Rstd[:, k, :], LnV[:, k, :], ACT.Exp, scale=-0.5).then_inc(s[out], 1)

            def stage1(b, u):
                rstd(b, 0, "mv1", "lnv1", "rstd1")
                wait(act, "cols", 2)
                wait(act, "xT1", b + 1)
                nc.scalar.activation(HT[:], psT[:], ACT.Identity, scale=Cols[:, 1, bass.ds(b, 1)],
                                     bias=Cols[:, 0, bass.ds(b, 1)]).then_inc(s["hT"], 1)
                wait(act, "uT_ps", b + 1)
                nc.scalar.copy(UT[:], pjA[0:LR, :]).then_inc(s["uT"], 1)
                wait(act, "q_ps", b + 1)
                wait(act, "qs", b)
                nc.scalar.mul(Q[:], pjB[:], float(HK ** -0.5)).then_inc(s["q_sb"], 1)
                wait(act, "gl_ps", b + 1)
                wait(act, "g16", b)
                nc.scalar.activation(GL[:], pjA[:], ACT.Identity, bias=Gb[:]).then_inc(s["gl_sb"], 1)
                wait(act, "gl_sb", b + 1)
                nc.scalar.activation(Ln1[:], GL[:], ACT.Abs).then_inc(s["abs1"], 1)
                wait(act, "abs1", b + 1)
                nc.scalar.activation(Ln1[:], Ln1[:], ACT.Exp, scale=-1.0).then_inc(s["ex1"], 1)
                wait(act, "ex1", b + 1)
                nc.scalar.activation(Ln1[:], Ln1[:], ACT.Ln, bias=1.0).then_inc(s["ln1"], 1)
                for c in (1, 3):
                    wait(act, "vg_ps", C * b + c + 1)
                    nc.scalar.copy(VG[u][:, c, :], pjB[:]).then_inc(s["vgB"], 1)
                wait(act, "difk", NS * b + NS)
                wait(act, "ktil", b)
                nc.scalar.activation(ExpK, DifK, ACT.Exp, scale=1.0 / GATE_NORM).then_inc(s["expk"], 1)
                wait(act, "difq", 2 * b + 2)
                wait(act, "qblk", H * b)
                wait(act, "kend", b)
                nc.scalar.activation(ExpQ[:], DifQ[:], ACT.Exp, scale=1.0 / GATE_NORM).then_inc(s["expq"], 1)
                nc.scalar.activation(ExpB[u][:], Cum[:], ACT.Exp, scale=1.0 / GATE_NORM).then_inc(s["expb"], 1)
                wait(act, "vgA", 2 * b + 2)
                wait(act, "vgB", 2 * b + 2)
                wait(act, "gate", b)
                g = VG[u][:, :, DV:]
                nc.scalar.activation(AbsG[:], g, ACT.Abs).then_inc(s["absg"], 1)
                wait(act, "absg", b + 1)
                nc.scalar.activation(AbsG[:], AbsG[:], ACT.Exp, scale=-1.0).then_inc(s["exg"], 1)
                wait(act, "exg", b + 1)
                nc.scalar.activation(AbsG[:], AbsG[:], ACT.Ln, bias=1.0).then_inc(s["lng"], 1)
                wait(act, "ming", b + 1)
                nc.scalar.activation(AbsG[:], AbsG[:], ACT.Exp).then_inc(s["sigg"], 1)

            def stage2(b, u):
                wait(act, "ket_ps", b + 1)
                nc.scalar.copy(KEt[:], psK[:, 0:3 * P].rearrange("p (c k) -> p c k", c=3)).then_inc(s["ket"], 1)
                for half in range(2):
                    wait(act, "o_ps", C * b + 2 * half + 2)
                    if half == 0:
                        wait(act, "ogat", b)
                    nc.scalar.copy(O[:, 2 * half:2 * half + 2, :],
                                   psO[:].rearrange("p (c v) -> p c v", c=2)).then_inc(s["o_sb"], 1)
                wait(act, "o_sb", 2 * b + 2)
                nc.scalar.activation(Sq[:], O[:], ACT.Square).then_inc(s["sq"], 1)
                wait(act, "ms", b + 1)
                nc.scalar.activation(Ms[:, 1, :], Ms[:, 0, :], ACT.Ln, scale=1.0 / HV, bias=EpsC[:]).then_inc(s["lnms"], 1)
                wait(act, "lnms", b + 1)
                nc.scalar.activation(Ms[:, 1, :], Ms[:, 1, :], ACT.Exp, scale=-0.5).then_inc(s["rms"], 1)
                wait(act, "oT_psa", b + 1)
                nc.scalar.copy(OT[:, 0, :], psS0[:]).then_inc(s["oTa"], 1)

            def stage3(b):
                rstd(b, 1, "mv2", "lnv2", "rstd2")
                wait(act, "xT2", b + 1)
                nc.scalar.copy(H2Tb[:], psT[:]).then_inc(s["h2T"], 1)
                wait(act, "h2T", b + 1)
                nc.scalar.copy(H2T[:, b, :], H2Tb[:]).then_inc(s["h2T_all"], 1)
                wait(act, "sh", b + 1)
                nc.scalar.activation(Sm[:, 1, :, :], Sm[:, 0, :, :], ACT.Exp).then_inc(s["ex"], 1)

            pipeline(act, stage1, stage2, stage3)

            with act.Fori(0, B) as n:
                for e in range(E):
                    for k in range(KH):
                        wait(act, "h_ps", n * (E * KH) + (e * KH + k + 1))
                        if k == 0 and e >= 2:
                            wait(act, "y_ps", n * E + (e - 1))
                        if k == 0 and e == 0:
                            wait(act, "y_ps", n * E)
                        nc.scalar.activation(GH[e % 2][:, k, :], psA[k][:], ACT.Gelu).then_inc(s["gelu"], 1)

        @block.vector
        def _(dve):
            v = nc.vector
            dve.wait_ge(s["silu_ln"], 1)
            v.scalar_tensor_tensor(SC[:, 3, :], CT[:], 0.0, SC[:, 2, :], ALU.min, ALU.subtract).then_inc(s["silu_min"], 1)
            dve.wait_ge(s["silu_sig"], 1)
            v.tensor_tensor(SilC[:], CT[:], SC[:, 3, :], ALU.mult).then_inc(s["silu_c"], 1)
            dve.wait_ge(s["silu_c"], 1)
            v.tensor_copy(SilB[:], SilC[:].rearrange("p (b o) -> p b o", o=1).to_broadcast([P, B, P])).then_inc(s["silu_b"], 1)
            for b in range(B):
                dve.wait_ge(s["rows_ps"], b + 1)
                v.tensor_copy(Rows[:, b, :, :], (pjA, pjB)[b % 2][:].rearrange("p (j d) -> p j d", j=4)).then_inc(s["rows"], 1)
            dve.wait_ge(s["rows"], B)
            for b in range(B):
                gates, sg, ab = Rows[:, b, 0:4:3, :], Sgn[:, b, 0:2, :], Sgn[:, b, 2:4, :]
                v.tensor_scalar(sg, gates, 0.0, 2.0, ALU.is_ge, ALU.mult).then_inc(s["rows_sgn"], 1)
                v.tensor_scalar(ab, gates, -1.0, None, ALU.mult).then_inc(s["rows_abs"], 1)
            dve.wait_ge(s["rows_abs"], B)
            for b in range(B):
                gates, ab = Rows[:, b, 0:4:3, :], Sgn[:, b, 2:4, :]
                v.scalar_tensor_tensor(ab, gates, 0.25, ab, ALU.max, ALU.max).then_inc(s["rows_mul"], 1)
            dve.wait_ge(s["rows_mul"], B)
            dve.wait_ge(s["rows_sgn"], B)
            for b in range(B):
                gates, sg, ab = Rows[:, b, 0:4:3, :], Sgn[:, b, 0:2, :], Sgn[:, b, 2:4, :]
                v.scalar_tensor_tensor(gates, sg, -1.0, ab, ALU.add, ALU.mult).then_inc(s["rows_used"], 1)
            v.tensor_scalar(Rows[:, :, 2, :], Rows[:, :, 2, :], 1.0, None, ALU.add).then_inc(s["rows_fin"], 1)
            dve.wait_ge(s["attn_in"], 64)
            v.tensor_scalar(Wo[:], WoR[:], RmsW[:], None, ALU.mult).then_inc(s["wo_fin"], 1)
            v.memset(HeadMask[:], 0.0).then_inc(s["hmask"], 1)
            dve.wait_ge(s["hmask"], 1)
            for h in range(H):
                v.memset(HeadMask[h * HK:(h + 1) * HK, h, :], 1.0).then_inc(s["hmask"], 1)
            dve.wait_ge(s["hmask"], 1 + H)
            dve.wait_ge(s["const"], 4)
            dve.wait_ge(s["zeroed"], 1)

            def norm(b, k, src, out, names):
                bn, mv, rs, done = names
                for c in range(C):
                    v.bn_stats(St6[:, k, c, :], src[:, b, c, :]).then_inc(s[bn], 1)
                wait(dve, bn, C * b + C)
                v.memset(Pad[:], 0.0)
                for c in range(C):
                    v.bn_aggr(MV[:, k, c, :], St6[:, k, c, :]).then_inc(s[mv], 1)
                wait(dve, rs, b + 1)
                for c in range(C):
                    v.tensor_scalar(out[:, c, :], src[:, b, c, :], MV[:, k, c, 0:1], Rstd[:, k, c:c + 1],
                                    ALU.subtract, ALU.mult).then_inc(s[done], 1)

            def stage1(b, u):
                dve.wait_ge(s[f"x_in{b}" if isinstance(b, int) and b < 2 else "x_in2"], 16)
                wait(dve, "xT1", b)
                norm(b, 0, X, Xh, ("bn1", "mv1", "rstd1", "xhat1"))
                wait(dve, "k_ps", b + 1)
                v.tensor_copy(K[:], pjB[:].rearrange("p (c t) -> p c t", c=C)).then_inc(s["k_sb"], 1)
                wait(dve, "ln1", b + 1)
                v.scalar_tensor_tensor(G16[:], GL[:], 0.0, Ln1[:], ALU.min, ALU.subtract).then_inc(s["g16"], 1)
                wait(dve, "g16", b + 1)
                wait(dve, "expb", b)
                v.tensor_tensor_scan(Cum[:].rearrange("p c i s -> p (c i s)"), Restart[:].rearrange("p c t -> p (c t)"),
                                     G16[:], 0.0, ALU.mult, ALU.add).then_inc(s["cum"], 1)
                for c in (0, 2):
                    wait(dve, "vg_ps", C * b + c + 1)
                    v.tensor_copy(VG[u][:, c, :], pjA[:]).then_inc(s["vgA"], 1)
                wait(dve, "cum", b + 1)
                wait(dve, "expk", b)
                for i in range(NS):
                    ref = Cum[:, :, i, SUB // 2 - 1:SUB // 2].to_broadcast([P, C, SUB * (i + 1)])
                    v.tensor_tensor(DifK[:, :, i, 0:SUB * (i + 1)], ref,
                                    Cum[:, :, 0:i + 1, :].rearrange("p c i s -> p c (i s)"), ALU.subtract).then_inc(s["difk"], 1)
                wait(dve, "expq", b)
                v.tensor_tensor(DifQ[:, 0, :].rearrange("p (c i s) -> p (c i) s", c=C, i=NS), Cum[:].rearrange("p c i s -> p (c i) s"),
                                Cum[:, :, :, SUB // 2 - 1:SUB // 2].rearrange("p c i s -> p (c i) s").to_broadcast([P, C * NS, SUB]),
                                ALU.subtract).then_inc(s["difq"], 1)
                v.tensor_tensor(DifQ[:, 1, :].rearrange("p (c t) -> p c t", c=C),
                                Cum[:, :, NS - 1, SUB - 1:SUB].to_broadcast([P, C, P]),
                                Cum[:].rearrange("p c i s -> p c (i s)"), ALU.subtract).then_inc(s["difq"], 1)
                wait(dve, "expk", b + 1)
                for c in range(C):
                    ins = v.tensor_tensor(KT[u][:, c, :, :], ExpK[:, c, :, :], K[:, c:c + 1, :].to_broadcast([P, NS, P]), ALU.mult)
                ins.then_inc(s["ktil"], 1)
                wait(dve, "expq", b + 1)
                v.tensor_tensor(KE[u][:], K[:], ExpQ[:, 1, :].rearrange("p (c t) -> p c t", c=C), ALU.mult).then_inc(s["kend"], 1)
                wait(dve, "qe", b + 1)
                for h in range(H):
                    v.tensor_scalar(QB[u][:, h, :], QE[:], HeadMask[:, h, 0:1], None, ALU.mult).then_inc(s["qblk"], 1)
                wait(dve, "lng", b + 1)
                v.scalar_tensor_tensor(AbsG[:], VG[u][:, :, DV:], 0.0, AbsG[:], ALU.min, ALU.subtract).then_inc(s["ming"], 1)

            def stage2(b, u):
                hm = HeadMask[:].rearrange("p h v -> p (h v)")
                cm = Causal[:].rearrange("p (o t) -> p o t", o=1).to_broadcast([P, H, P])

                def scores(c):
                    wait(dve, "sc_ps", C * b + c + 1)
                    if c >= 2:
                        wait(dve, "o_ps", C * b + c - 1)
                    v.tensor_tensor(PT[c % 2][:], (psS0, psS1)[c % 2][:].rearrange("p (h t) -> p h t", h=H), cm,
                                    ALU.mult).then_inc(s["pt"], 1)

                def state(c):
                    if c == 0:
                        v.tensor_tensor(S[0][:], psD[:, 0:DV], hm, ALU.mult).then_inc(s["s_st"], 1)
                        return
                    src = psD[:, DV:2 * DV] if c == 1 else psK[:, 0:DV]
                    v.tensor_tensor(Stmp[:, c - 1, :], src, hm, ALU.mult).then_inc(s["s_tmp"], 1)
                    wait(dve, "s_tmp", 2 * b + c)
                    wait(dve, "s_st", 3 * b + c)
                    v.scalar_tensor_tensor(S[c][:], S[c - 1][:], ExpB[u][:, c * P + P - 1:c * P + P], Stmp[:, c - 1, :],
                                           ALU.mult, ALU.add).then_inc(s["s_st"], 1)

                scores(0)
                scores(1)
                wait(dve, "ds_ps", b + 1)
                for c in range(3):
                    state(c)
                scores(2)
                scores(3)
                wait(dve, "sq", b + 1)
                v.tensor_reduce(Ms[:, 0, :], Sq[:].rearrange("p c (h v) -> p (c h) v", h=H), axis=AX.X, op=ALU.add).then_inc(s["ms"], 1)
                wait(dve, "rms", b + 1)
                v.tensor_tensor(O[:].rearrange("p c (h v) -> p (c h) v", h=H), O[:].rearrange("p c (h v) -> p (c h) v", h=H),
                                Ms[:, 1, :].rearrange("p (n o) -> p n o", o=1).to_broadcast([P, C * H, HV]), ALU.mult).then_inc(s["onrm"], 1)
                wait(dve, "onrm", b + 1)
                wait(dve, "gate", b + 1)
                v.tensor_tensor(O[:], O[:], Gate[u], ALU.mult).then_inc(s["ogat"], 1)
                wait(dve, "oT_psb", b + 1)
                v.tensor_copy(OT[:, 1, :], psS1[:]).then_inc(s["oTb"], 1)
                wait(dve, "at_ps", b + 1)
                wait(dve, "x2", b)
                v.tensor_tensor(At[:], psO[:].rearrange("p (c d) -> p c d", c=C), Rows[:, b, 0:1, :].to_broadcast([P, C, D]),
                                ALU.mult).then_inc(s["at_g"], 1)

            def stage3(b):
                wait(dve, "x2", b + 1)
                wait(dve, "xT2", b)
                norm(b, 1, X2, H2, ("bn2", "mv2", "rstd2", "xhat2"))
                wait(dve, "lg_ps", b + 1)
                v.tensor_copy(LG[:], psT[:, 0:C * E].rearrange("p (c e) -> p c e", c=C)).then_inc(s["lg"], 1)
                wait(dve, "lg", b + 1)
                for c in range(C):
                    mine = LG[:, c, :].rearrange("p (e o) -> p e o", o=1).to_broadcast([P, E, E])
                    other = LG[:, c:c + 1, :].to_broadcast([P, E, E])
                    v.tensor_tensor(Rk[:, 0, c, :, :], other, mine, ALU.is_gt).then_inc(s["rk0"], 1)
                    v.tensor_tensor(Rk[:, 1, c, :, :], other, mine, ALU.is_equal).then_inc(s["rk1"], 1)
                v.tensor_reduce(R1[:, 0, :], LG[:], axis=AX.X, op=ALU.max).then_inc(s["mx"], 1)
                wait(dve, "rk1", C * b + C)
                bf = Before[:].rearrange("p e j -> p (e j)").rearrange("p (o n) -> p o n", o=1).to_broadcast([P, C, E * E])
                rk = [Rk[:, j, :, :, :].rearrange("p c e j -> p c (e j)") for j in range(3)]
                v.tensor_tensor(rk[1], rk[1], bf, ALU.mult).then_inc(s["rk2"], 1)
                wait(dve, "mx", b + 1)
                v.tensor_tensor(Sm[:, 0, :, :], LG[:], R1[:, 0, :].rearrange("p (c o) -> p c o", o=1).to_broadcast([P, C, E]),
                                ALU.subtract).then_inc(s["sh"], 1)
                wait(dve, "rk2", b + 1)
                wait(dve, "rk0", C * b + C)
                v.tensor_tensor(rk[0], rk[0], rk[1], ALU.add).then_inc(s["rk3"], 1)
                wait(dve, "rk3", b + 1)
                v.tensor_reduce(Sm[:, 2, :, :].rearrange("p c e -> p (c e)"), Rk[:, 0, :, :, :].rearrange("p c e j -> p (c e) j"),
                                axis=AX.X, op=ALU.add).then_inc(s["rk4"], 1)
                wait(dve, "ex", b + 1)
                v.tensor_reduce(R1[:, 1, :], Sm[:, 1, :, :], axis=AX.X, op=ALU.add).then_inc(s["sum"], 1)
                wait(dve, "sum", b + 1)
                v.reciprocal(R1[:, 2, :], R1[:, 1, :]).then_inc(s["rsum"], 1)
                wait(dve, "rsum", b + 1)
                v.tensor_tensor(Sm[:, 3, :, :], Sm[:, 1, :, :], R1[:, 2, :].rearrange("p (c o) -> p c o", o=1).to_broadcast([P, C, E]),
                                ALU.mult).then_inc(s["pr"], 1)
                wait(dve, "pr", b + 1)
                wait(dve, "rk4", b + 1)
                v.scalar_tensor_tensor(WGT[:, b, :, :], Sm[:, 2, :, :], 1.5, Sm[:, 3, :, :], ALU.is_lt, ALU.mult).then_inc(s["wgt"], 1)

            pipeline(dve, stage1, stage2, stage3)

            dve.wait_ge(s["wgt"], B)
            with dve.Fori(0, B) as n:
                for e in range(E):
                    wait(dve, "y_ps", n * E + (e + 1))
                    for c in range(C):
                        y = psA[4 + e % 2][:, c * D:(c + 1) * D]
                        w = WGT[:, n, c, e:e + 1]
                        if e == 0:
                            v.tensor_scalar(Acc[:, c, :], y, w, None, ALU.mult).then_inc(s["acc"], 1)
                        else:
                            wait(dve, "acc", n * (E * C) + (e * C - C + c + 1))
                            v.scalar_tensor_tensor(Acc[:, c, :], y, w, Acc[:, c, :], ALU.mult, ALU.add).then_inc(s["acc"], 1)
                wait(dve, "acc", n * (E * C) + E * C)
                wait(dve, "out_dma", n * 16)
                v.tensor_tensor(Yo[:], Acc[:], Rows[:, n, 3:4, :].to_broadcast([P, C, D]), ALU.mult).then_inc(s["y_gb"], 1)
                wait(dve, "y_gb", n + 1)
                v.tensor_tensor(Yo[:], Yo[:], X2[:, n, :, :], ALU.add).then_inc(s["y_fin"], 1)

        @block.tensor
        def _(pe):
            mm = nc.tensor.matmul
            pe.wait_ge(s["wmod_in"], 16)
            pe.wait_ge(s["silu_c"], 1)
            for j in range(2):
                ins = mm(psT[:, j * B:(j + 1) * B], Wmod[:, j * D:(j + 1) * D], SilC[:], start=True, stop=True)
            ins.then_inc(s["cols_ps"], 1)
            pe.wait_ge(s["silu_b"], 1)
            for b in range(B):
                if b >= 2:
                    pe.wait_ge(s["rows"], b - 1)
                mm((pjA, pjB)[b % 2][:], SilB[:, b, :], Wmod[:, 2 * D:6 * D], start=True, stop=True).then_inc(s["rows_ps"], 1)
            pe.wait_ge(s["ident"], 1)
            pe.wait_ge(s["proj_in"], 96)
            pe.wait_ge(s["cols"], 2)
            pe.wait_ge(s["rows"], B)

            def stage1(b, u):
                wait(pe, "xhat1", C * b + C)
                wait(pe, "lg", b - 2)
                for c in range(C):
                    ins = nc.tensor.transpose(psT[:, c * P:(c + 1) * P], Xh[:, c, :], Id[:])
                ins.then_inc(s["xT1"], 1)
                wait(pe, "hT", b + 1)
                wait(pe, "vgA", 2 * b)
                wait(pe, "vgB", 2 * b)
                mm(pjA[0:LR, :], W1k[:], HT[:], start=True, stop=True).then_inc(s["uT_ps"], 1)
                mm(pjB[:], Wq[:], HT[:], start=True, stop=True).then_inc(s["q_ps"], 1)
                wait(pe, "uT", b + 1)
                mm(pjA[:], W2k[:], UT[:], start=True, stop=True).then_inc(s["gl_ps"], 1)
                wait(pe, "q_sb", b + 1)
                mm(pjB[:], Wk[:], HT[:], start=True, stop=True).then_inc(s["k_ps"], 1)
                for c in range(C):
                    if c == 0:
                        wait(pe, "gl_sb", b + 1)
                    elif c == 1:
                        wait(pe, "k_sb", b + 1)
                    elif c == 2:
                        wait(pe, "vgA", 2 * b + 1)
                    else:
                        wait(pe, "vgB", 2 * b + 1)
                    mm((pjA, pjB)[c % 2][:], HT[:, c * P:(c + 1) * P], Wvg[:], start=True, stop=True).then_inc(s["vg_ps"], 1)

            def stage2(b, u):
                wait(pe, "kend", b + 1)
                wait(pe, "s_st", 3 * b)
                for c in range(3):
                    ins = nc.tensor.transpose(psK[:, c * P:(c + 1) * P], KE[u][:, c, :], Id[:])
                ins.then_inc(s["ket_ps"], 1)
                wait(pe, "ktil", b + 1)
                wait(pe, "qblk", H * b + H)
                wait(pe, "oTa", b)
                wait(pe, "oTb", b)

                def scores(c):
                    if c >= 2:
                        wait(pe, "pt", C * b + c - 1)
                    ps = (psS0, psS1)[c % 2][:].rearrange("p (h i t) -> p h i t", h=H, i=NS)
                    for i in range(NS):
                        t0 = c * P + i * SUB
                        ins = mm(ps[:, :, i, :], KT[u][:, c, i, :], QB[u][:, :, t0:t0 + SUB], start=True, stop=True)
                    ins.then_inc(s["sc_ps"], 1)

                def output(c):
                    o = psO[:, (c % 2) * DV:(c % 2 + 1) * DV]
                    wait(pe, "pt", C * b + c + 1)
                    if c:
                        wait(pe, "s_st", 3 * b + c)
                        mm(o, QS[u][:, c * P:(c + 1) * P], S[c - 1][:], start=True, stop=False, skip_group_check=True)
                    for h in range(H):
                        ins = mm(o[:, h * HV:(h + 1) * HV], PT[c % 2][:, h, :], VG[u][:, c, h * HV:(h + 1) * HV],
                                 start=(c == 0), stop=(c == 0 or h == H - 1), skip_group_check=True)
                    ins.then_inc(s["o_ps"], 1)

                scores(0)
                scores(1)
                wait(pe, "ket", b + 1)
                wait(pe, "vgA", 2 * b + 2)
                wait(pe, "vgB", 2 * b + 2)
                for c in range(3):
                    ds = psD[:, c * DV:(c + 1) * DV] if c < 2 else psK[:, 0:DV]
                    ins = mm(ds, KEt[:, c, :], VG[u][:, c, 0:DV], start=True, stop=True)
                ins.then_inc(s["ds_ps"], 1)
                wait(pe, "qs", b + 1)
                wait(pe, "at_g", b)
                output(0)
                output(1)
                scores(2)
                scores(3)
                wait(pe, "o_sb", 2 * b + 1)
                output(2)
                output(3)
                wait(pe, "ogat", b + 1)
                wait(pe, "pt", C * b + C)
                for j, ps in enumerate((psS0, psS1)):
                    for c in range(C):
                        ins = nc.tensor.transpose(ps[:, c * P:(c + 1) * P], O[:, c, j * P:(j + 1) * P], Id[:])
                    ins.then_inc(s["oT_psa" if j == 0 else "oT_psb"], 1)
                wait(pe, "wo_fin", 1)
                wait(pe, "oTa", b + 1)
                wait(pe, "oTb", b + 1)
                wait(pe, "o_sb", 2 * b + 2)
                for c in range(C):
                    for j in range(2):
                        ins = mm(psO[:, c * P:(c + 1) * P], OT[:, j, c * P:(c + 1) * P], Wo[:, j, :],
                                 start=(j == 0), stop=(j == 1))
                ins.then_inc(s["at_ps"], 1)

            def stage3(b):
                wait(pe, "h2", b + 1)
                for c in range(C):
                    ins = nc.tensor.transpose(psT[:, c * P:(c + 1) * P], H2[:, c, :], Id[:])
                ins.then_inc(s["xT2"], 1)
                wait(pe, "h2T", b + 1)
                wait(pe, "attn_in", 64)
                for c in range(C):
                    ins = mm(psT[:, c * E:(c + 1) * E], H2Tb[:, c * P:(c + 1) * P], Rw[:], start=True, stop=True)
                ins.then_inc(s["lg_ps"], 1)

            pipeline(pe, stage1, stage2, stage3)

            pe.wait_ge(s["ffn_in"], 32)
            pe.wait_ge(s["lg"], B)
            pe.wait_ge(s["h2T_all"], B)
            pe.wait_ge(s["at_g"], B)
            n_h = E * KH
            with pe.Fori(0, B) as n:
                def hidden(e):
                    for k in range(KH):
                        wait(pe, "gelu", n * n_h + (e * KH - KH + k + 1) if e else n * n_h)
                        mm(psA[k][:], W1[:, e, k * P:(k + 1) * P], H2T[:, n, :], start=True, stop=True).then_inc(s["h_ps"], 1)

                def down(e):
                    wait(pe, "gelu", n * n_h + (e * KH + KH))
                    wait(pe, "acc", n * (E * C) + (e - 1) * C if e >= 1 else n * (E * C))
                    for c in range(C):
                        for k in range(KH):
                            ins = mm(psA[4 + e % 2][:, c * D:(c + 1) * D], GH[e % 2][:, k, c * P:(c + 1) * P], W2[:, e, k, :],
                                     start=(k == 0), stop=(k == KH - 1))
                    ins.then_inc(s["y_ps"], 1)

                hidden(0)
                for e in range(1, E):
                    hidden(e)
                    down(e - 1)
                down(E - 1)


_INS = ["x", "cT", "wmod", "wq", "wk", "wvg", "gk_w1", "gk_w2", "gk_b", "wo", "rms_w", "rwT", "w1T", "w2T"]


def kernel(**inputs):
    import concourse.bacc as bacc
    from concourse.bass_utils import run_bass_kernel_spmd

    i = {k.removeprefix("L0_"): np.asarray(v) for k, v in inputs.items()}
    laid = {
        "x": i["attn_x"],
        "cT": i["c"].T,
        "wmod": i["wmod"],
        "wq": i["attn_Wq"],
        "wk": i["attn_Wk"],
        "wvg": np.concatenate([i["attn_Wv"], i["attn_Wg"]], axis=1),
        "gk_w1": i["attn_gk_w1"],
        "gk_w2": i["attn_gk_w2"],
        "gk_b": i["attn_gk_b"].reshape(DK, 1),
        "wo": i["attn_Wo"].reshape(2, P, D).transpose(1, 0, 2),
        "rms_w": i["attn_rms_w"].reshape(HV, 1),
        "rwT": i["ffn_router_w"].T,
        "w1T": i["ffn_w1"].transpose(2, 0, 1),
        "w2T": i["ffn_w2"].reshape(E, D, KH, P).transpose(3, 0, 2, 1),
    }
    nc = bacc.Bacc("TRN2", target_bir_lowering=False, num_devices=1)
    arrays, args = {}, []
    for name in _INS:
        a = np.ascontiguousarray(laid[name])
        arrays[f"in_{name}"] = a
        args.append(nc.dram_tensor(f"in_{name}", a.shape, mybir.dt.from_np(a.dtype), kind="ExternalInput").ap())
    args.append(nc.dram_tensor("out", (B, T, D), F32, kind="ExternalOutput").ap())
    build_program(nc, *args)
    r = run_bass_kernel_spmd(nc, [arrays], core_ids=[0])
    return r.results[0]["out"]
```

```python
from contextlib import ExitStack

import numpy as np

import concourse.bass as bass
from concourse import mybir

F32 = mybir.dt.float32
F32R = mybir.dt.float32r
I32, U32 = mybir.dt.int32, mybir.dt.uint32
ALU = mybir.AluOpType
ACT = mybir.ActivationFunctionType
AX = mybir.AxisListType

P = 128
B, T, D = 8, 512, 128
H, HK, HV = 4, 32, 64
DK, DV = H * HK, H * HV
LR = 16
C = T // P
SUB = 32
NS = P // SUB
E, HID = 8, 512
KH = HID // P
EPS = 1e-5
GATE_NORM = 16.0
MODS = 6
N = B * T
TOP = 2
BT = 256
BH = BT // P
REG = N + BT
SPARE = E * REG
ROWS = SPARE + BT
RING = 4
NBLK = -(-((TOP * N + E * (BT - 1)) // BT) // RING) * RING
RW = D + 1


def build_program(nc, x, cT, wmod, wq, wk, wvg, gk_w1, gk_w2, gk_b, wo, rms_w, rwT, w1T, w2T, out):
    rows_dram = nc.dram_tensor("expert_rows", (ROWS, RW), F32, kind="Internal").ap()
    y_dram = nc.dram_tensor("expert_out", (TOP * N, D), F32, kind="Internal").ap()
    with ExitStack() as ctx:
        def sb(name, shape, dt=F32):
            return ctx.enter_context(nc.sbuf_tensor(name, shape, dt))

        def bank(name):
            return ctx.enter_context(nc.psum_tensor(name, [P, 512], F32))

        def sem(name):
            return ctx.enter_context(nc.semaphore(name))

        W1hi, W1lo = (sb(n, [P, E, HID], F32R) for n in ("W1hi", "W1lo"))
        W2hi, W2lo = (sb(n, [P, E, HID], F32R) for n in ("W2hi", "W2lo"))
        Id = sb("Id", [P, P])
        X = sb("X", [P, B, C, D])
        GBr = sb("GBr", [P, B, D])
        W01 = sb("W01", [P, B, TOP, C])
        Count = sb("Count", [P, C + 1, E])
        PadP = sb("PadP", [P, 1])
        PadRow = sb("PadRow", [P, BH, RW])
        Tab = sb("Tab", [P, 2, NBLK], I32)
        PadAt = sb("PadAt", [P, E], I32)

        a_ctx = ExitStack()

        def sa(name, shape, dt=F32):
            return a_ctx.enter_context(nc.sbuf_tensor(name, shape, dt))

        Stage = sa("Stage", [P, 2, HID])
        Wmod = sa("Wmod", [P, MODS * D])
        CT = sa("CT", [P, B])
        Wq, Wk = sa("Wq", [P, DK]), sa("Wk", [P, DK])
        Wvg = sa("Wvg", [P, 2 * DV])
        W1k, W2k = sa("W1k", [P, LR]), sa("W2k", [LR, DK])
        Gb = sa("Gb", [P, 1])
        Wo = sa("Wo", [P, 2, D])
        RmsW = sa("RmsW", [P, 1])
        Rw = sa("Rw", [P, E])
        Causal = sa("Causal", [P, P])
        Earlier = sa("Earlier", [P, P])
        Ones = sa("Ones", [P, P])
        HeadMask = sa("HeadMask", [P, H, HV])
        Restart = sa("Restart", [P, C, P], mybir.dt.bfloat16)
        Before = sa("Before", [P, E, E])
        EpsC = sa("EpsC", [P, 1])
        Place = sa("Place", [P, B, TOP, C], I32)
        RegE = sa("RegE", [P, E])
        Jn = sa("Jn", [P, NBLK])
        SC = sa("SC", [P, 4, B])
        SilC = sa("SilC", [P, B])
        SilB = sa("SilB", [P, P])
        Cols = sa("Cols", [P, 2, B])
        Rows = [sa(f"Rows{u}", [P, 4, D]) for u in range(2)]
        St6 = sa("St6", [P, 2, C, 6])
        Pad = sa("Pad", [P, 1])
        MV = sa("MV", [P, 2, C, 2])
        LnV, Rstd = sa("LnV", [P, 2, C]), sa("Rstd", [P, 2, C])
        Xh = sa("Xh", [P, C, D])             
        HT = sa("HT", [P, T])
        H2T = sa("H2T", [P, T])
        UT = sa("UT", [LR, T])
        Q, K = sa("Q", [P, T]), sa("K", [P, C, P])
        GL, Ln1 = sa("GL", [P, T]), sa("Ln1", [P, T])
        Cum = sa("Cum", [P, C, NS, SUB])
        ExpQ = sa("ExpQ", [P, 2, T])
        ExpB = sa("ExpB", [P, T])
        Decay = sa("Decay", [P, C])
        KT = sa("KT", [P, C, NS, P])
        KE = sa("KE", [P, C, P])
        QE = sa("QE", [P, T])
        WoR = QE[:, 0:2 * D].rearrange("p (j d) -> p j d", j=2)
        QB = sa("QB", [P, H, T])
        QS = sa("QS", [P, T])
        VG = sa("VG", [P, C, 2 * DV])
        AbsG = sa("AbsG", [P, C, DV])
        Gate = VG[:, :, DV:]
        KEt = sa("KEt", [P, 3, P])
        PT = [sa(f"PT{i}", [P, H, P]) for i in range(2)]
        S = [sa(f"S{c}", [P, DV]) for c in range(3)]
        Stmp = sa("Stmp", [P, 2, DV])
        Sgn = Stmp[:].rearrange("p a v -> p (a v)").rearrange("p (j d) -> p j d", j=4)
        O = sa("O", [P, C, DV])
        Ms = sa("Ms", [P, 2, C * H])
        OT = sa("OT", [P, 2, T])
        Sq = OT[:].rearrange("p j t -> p (j t)").rearrange("p (c v) -> p c v", c=C)
        At = sa("At", [P, C, D])
        H2 = sa("H2", [P, C, D])
        HR = sa("HR", [P, TOP, C, RW])
        LG = sa("LG", [P, C, E])
        Rk = sa("Rk", [P, 2, C, E, E])
        Sm = sa("Sm", [P, 4, C, E])
        Sel = sa("Sel", [P, C, E])
        Sel2 = sa("Sel2", [P, TOP, C, E])
        Pick = sa("Pick", [P, 2, TOP, C, E])
        Slot = sa("Slot", [P, TOP, C])
        SlotI = sa("SlotI", [P, TOP, C], U32)
        R1 = sa("R1", [P, 4, C])
        Nb = sa("Nb", [P, 4, E])
        NbI = sa("NbI", [P, 2, E], I32)
        Le = Stage[:].rearrange("p a n -> p (a n)")[:, 0:2 * NBLK * E].rearrange("p (a j e) -> p a j e", a=2, e=E)
        Bl = sa("Bl", [P, 4, NBLK])
        a_ctx.close()
        XR = [sb(f"XR{r}", [P, BH, RW]) for r in range(RING)]
        Ids = [sb(f"Ids{r}", [P, BH], U32) for r in range(RING)]
        XThi = [sb(f"XThi{u}", [P, BT], F32R) for u in range(2)]
        XTlo = [sb(f"XTlo{u}", [P, BT], F32R) for u in range(2)]
        G = [sb(f"G{u}", [P, BH, HID]) for u in range(2)]
        GThi = [sb(f"GThi{u}", [P, BH, KH, P], F32R) for u in range(2)]
        GTlo = [sb(f"GTlo{u}", [P, BH, KH, P], F32R) for u in range(2)]
        YS = [sb(f"YS{r}", [P, BH, D]) for r in range(RING)]
        Y = sb("Y", [P, B, TOP, C, D])

        psA = [bank(f"ps{i}") for i in range(8)]
        psT, pjA, pjB, psS0, psS1, psK, psD, psO = psA
        psX, psH, psG, psY = psA[0], (psA[1:3], psA[3:5]), psA[5:7], psA[7]

        names = ("c_in wmod_in proj_in attn_in ident_a ident const silu_b cols_ps cols rows_ps rows rows_used rows_mul "
                 "rows_fin wo_fin bn1 mv1 lnv1 rstd1 xhat1 xT1 hT uT_ps uT q_ps q_sb gl_ps gl_sb k_ps k_sb vg_ps abs1 "
                 "ex1 ln1 g16 cum difk difq expk expq expb ktil qe hmask qblk qs absg exg lng ming sigg gate ket_ps "
                 "ket sc_ps pt ds_ps s_tmp s_st o_ps o_sb sq ms lnms rms onrm ogat at_ps at_g x2 bn2 mv2 lnv2 rstd2 "
                 "xhat2 h2 xT2 h2T lg_ps lg row_h row_id rk4 sh ex sel sel2 carry count pos_ps slot w01 slotu scat "
                 "stage w_hi w_lo cnt_ps ce tab_row tab_e pad_at padrow pads table gb_row decay xt_ps xt_hi xt_lo h_ps "
                 "gelu gt_ps gt_hi gt_lo y_ps ys yw0 yw ygb yfin out_dma silu_act silu_dve rk01 rows_ab oT_ps held "
                 "xin0 xin1 route ids xblk0 xblk1 xblk2 xblk3 ysc0 ysc1 ysc2 ysc3 xin2 vg oT ").split()
        names += [f"y_in{b}" for b in range(B)]
        s = {n: sem(n) for n in names}

        def wait(eng, name, value):
            if isinstance(value, int) and value <= 0:
                return
            eng.wait_ge(s[name], value)

        block = ctx.enter_context(nc.Block())

        ORDER = ("p2_scores p1_norm p3_norm p2_state p1_transpose p3_rows p2_output p1_query p3_logits p2_rms p1_gates "
                 "p3_rank p1_values p2_transpose p1_differences p3_slots p2_project p1_keys p3_scatter p1_outgate").split()

        def pipeline(eng, **piece):
            def run(which, b, u):
                for name in ORDER:
                    if name[1] in which and name in piece:
                        piece[name](b + {"1": 1, "2": 0, "3": -1}[name[1]], u if name[1] == "2" else 1 - u)

            run("1", -1, 1)
            run("12", 0, 0)
            with eng.Fori(0, (B - 2) // 2) as i:
                run("123", i * 2 + 1, 1)
                run("123", i * 2 + 2, 0)
            run("23", B - 1, 1)
            run("3", B, 0)

        def block_pipeline(a, b, c1, c2):
            def step(j, r, turn, rest):
                if rest >= 2:
                    a(j + 2, (r + 2) % RING, turn + (r + 2) // RING)
                c1(j, r, turn)
                if rest >= 1:
                    b(j + 1, (r + 1) % RING, turn + (r + 1) // RING)
                c2(j, r, turn)

            a(0, 0, 0)
            a(1, 1, 0)
            b(0, 0, 0)
            return step

        def run_blocks(eng, step):
            with eng.Fori(0, NBLK // RING - 1) as i:
                for r in range(RING):
                    step(i * RING + r, r, i, 2)
            for r in range(RING):
                step(NBLK - RING + r, r, NBLK // RING - 1, RING - 1 - r)

        @block.sync
        def _(sp):
            xv = x.rearrange("b (c p) d -> p b c d", p=P)
            sp.dma_start(CT[:], cT).then_inc(s["c_in"], 16)
            sp.dma_start(X[:, 0, :, :], xv[:, 0, :, :]).then_inc(s["xin0"], 16)
            sp.dma_start(Wmod[:], wmod).then_inc(s["wmod_in"], 16)
            for dst, src in ((Wq, wq), (Wk, wk), (Wvg, wvg), (W1k, gk_w1), (W2k, gk_w2), (Gb, gk_b)):
                sp.dma_start(dst[:], src).then_inc(s["proj_in"], 16)
            sp.dma_start(X[:, 1, :, :], xv[:, 1, :, :]).then_inc(s["xin1"], 16)
            sp.dma_start(X[:, 2:, :, :], xv[:, 2:, :, :]).then_inc(s["xin2"], 16)
            sp.dma_start(WoR, wo).then_inc(s["attn_in"], 16)
            sp.dma_start(Rw[:], rwT).then_inc(s["attn_in"], 16)
            for j in range(2):
                sp.dma_start(RmsW[j * HV:(j + 1) * HV, :], rms_w).then_inc(s["attn_in"], 16)

            def stage_weights(e):
                sp.dma_start(Stage[:, 0, :], w1T[:, e, :]).then_inc(s["stage"], 16)
                sp.dma_start(Stage[:, 1, :], w2T[:, e, :]).then_inc(s["stage"], 16)

            stage_weights(0)
            with sp.Fori(0, E - 1) as e:
                wait(sp, "w_lo", e * 2 + 2)
                stage_weights(e + 1)
            sp.wait_ge(s["padrow"], 2)
            pad = PadRow[:]
            sp.dma_start(rows_dram[SPARE:SPARE + BT, :].rearrange("(j p) d -> p j d", p=P), pad).then_inc(s["pads"], 16)
            sp.wait_ge(s["pad_at"], 1)
            for e in range(E):
                at = sp.value_load(PadAt[0:1, e:e + 1], min_val=e * REG, max_val=e * REG + N)
                sp.dma_start(rows_dram[bass.ds(at, BT), :].rearrange("(j p) d -> p j d", p=P), pad).then_inc(s["pads"], 16)
            sp.wait_ge(s["pads"], 16 * (E + 1))
            sp.wait_ge(s["scat"], 16 * TOP * C * B)

            def load(j, r):
                at = sp.value_load(Tab[0:1, 0, bass.ds(j, 1)], min_val=0, max_val=SPARE)
                sp.dma_start(XR[r][:], rows_dram[bass.ds(at, BT), :].rearrange("(j p) d -> p j d", p=P)).then_inc(s[f"xblk{r}"], 16)

            sp.wait_ge(s["tab_row"], 1)
            sp.wait_ge(s["slotu"], B)
            for r in range(RING):
                load(r, r)
            with sp.Fori(0, NBLK // RING - 1) as i:
                for r in range(RING):
                    wait(sp, "xt_ps", i * RING + (r + 1))
                    wait(sp, "ids", i * RING + (r + 1))
                    load(i * RING + (RING + r), r)
            for r in range(RING):
                sp.wait_ge(s[f"ysc{r}"], 16 * BH * NBLK // RING)
            yv = y_dram.rearrange("(k b c p) d -> p b k c d", p=P, c=C, b=B)
            for b in range(B):
                for k in range(TOP):
                    sp.dma_start(Y[:, b, k, :, :], yv[:, b, k, :, :]).then_inc(s[f"y_in{b}"], 16)
            ov = out.rearrange("b (c p) d -> p b c d", p=P)
            for b in range(B):
                sp.wait_ge(s["yfin"], b + 1)
                sp.dma_start(ov[:, b, :, :], X[:, b, :, :]).then_inc(s["out_dma"], 16)
            sp.wait_ge(s["out_dma"], 16 * B)

        @block.gpsimd
        def _(pool):
            nc.gpsimd.memset(Id[:], 0.0).then_inc(s["ident_a"], 1)
            nc.gpsimd.memset(Causal[:], 1.0).then_inc(s["ident_a"], 1)
            nc.gpsimd.memset(Earlier[:], 1.0).then_inc(s["ident_a"], 1)
            nc.gpsimd.memset(Restart[:], 1.0).then_inc(s["ident_a"], 1)
            nc.gpsimd.memset(Before[:], 1.0).then_inc(s["ident_a"], 1)
            nc.gpsimd.memset(EpsC[:], EPS).then_inc(s["const"], 1)
            nc.gpsimd.memset(Ones[:], 1.0).then_inc(s["const"], 1)
            pool.wait_ge(s["ident_a"], 5)
            nc.gpsimd.affine_select(out=Id[:], in_=Id[:], compare_op=ALU.not_equal, fill=1.0, base=0,
                                    pattern=[[-1, P]], channel_multiplier=1).then_inc(s["ident"], 1)
            nc.gpsimd.affine_select(out=Causal[:], in_=Causal[:], compare_op=ALU.is_ge, fill=0.0, base=0,
                                    pattern=[[1, P]], channel_multiplier=-1).then_inc(s["const"], 1)
            nc.gpsimd.affine_select(out=Earlier[:], in_=Earlier[:], compare_op=ALU.is_gt, fill=0.0, base=0,
                                    pattern=[[1, P]], channel_multiplier=-1).then_inc(s["const"], 1)
            nc.gpsimd.memset(Restart[:, :, 0:1], 0.0).then_inc(s["const"], 1)
            nc.gpsimd.affine_select(out=Before[:], in_=Before[:], compare_op=ALU.is_gt, fill=0.0, base=0,
                                    pattern=[[1, E], [-1, E]], channel_multiplier=0).then_inc(s["const"], 1)
            nc.gpsimd.iota(Place[:], pattern=[[T, B], [N, TOP], [P, C]], base=0, channel_multiplier=1).then_inc(s["const"], 1)
            nc.gpsimd.iota(RegE[:], pattern=[[REG, E]], base=0, channel_multiplier=0,
                           allow_small_or_imprecise_dtypes=True).then_inc(s["const"], 1)
            nc.gpsimd.iota(Jn[:], pattern=[[1, NBLK]], base=0, channel_multiplier=0,
                           allow_small_or_imprecise_dtypes=True).then_inc(s["const"], 1)
            nc.gpsimd.memset(KT[:], 0.0).then_inc(s["const"], 1)
            nc.gpsimd.memset(Count[:], 0.0).then_inc(s["const"], 1)
            nc.gpsimd.memset(PadRow[:], 0.0).then_inc(s["padrow"], 1)
            pool.wait_ge(s["padrow"], 1)
            nc.gpsimd.iota(PadRow[:, :, D:RW].bitcast(I32), pattern=[[P, BH], [0, 1]], base=TOP * N,
                           channel_multiplier=1).then_inc(s["padrow"], 1)

            def carry_wait():
                nc.gpsimd.tensor_tensor(PadP[:], Id[:, 0:1], Id[:, 0:1], ALU.mult).then_inc(s["held"], 1)

            def keys(b, u):
                wait(pool, "wo_fin", 1)
                wait(pool, "expq", 2 * b + 2)
                wait(pool, "q_sb", b + 1)
                wait(pool, "qblk", H * b)
                nc.gpsimd.tensor_tensor(QE[:], Q[:], ExpQ[:, 0, :], ALU.mult).then_inc(s["qe"], 1)
                wait(pool, "expb", b + 1)
                wait(pool, "o_ps", C * b)
                nc.gpsimd.tensor_tensor(QS[:], Q[:], ExpB[:], ALU.mult).then_inc(s["qs"], 1)

            def outgate(b, u):
                wait(pool, "sigg", b + 1)
                nc.gpsimd.tensor_tensor(Gate, Gate, AbsG[:], ALU.mult).then_inc(s["gate"], 1)

            def low_parts(b, u):
                wait(pool, "w_hi", 2 * b + 2)
                nc.gpsimd.tensor_tensor(W1lo[:, b, :], Stage[:, 0, :], W1hi[:, b, :].bitcast(F32), ALU.subtract).then_inc(s["w_lo"], 1)
                nc.gpsimd.tensor_tensor(W2lo[:, b, :], Stage[:, 1, :], W2hi[:, b, :].bitcast(F32), ALU.subtract).then_inc(s["w_lo"], 1)

            def project(b, u):
                wait(pool, "at_g", b + 1)
                nc.gpsimd.tensor_tensor(X[:, b, :, :], X[:, b, :, :], At[:], ALU.add).then_inc(s["x2"], 1)

            def rows(b, u):
                wait(pool, "xhat2", b * C + C)
                wait(pool, "rows_fin", b + 1)
                nc.gpsimd.tensor_tensor(H2[:], H2[:], Rows[u][:, 2:3, :].to_broadcast([P, C, D]), ALU.mult).then_inc(s["h2"], 1)
                wait(pool, "h2", 2 * b + 1)
                nc.gpsimd.tensor_tensor(H2[:], H2[:], Rows[u][:, 1:2, :].to_broadcast([P, C, D]), ALU.add).then_inc(s["h2"], 1)

            def scatter(b, u):
                wait(pool, "held", b)
                wait(pool, "slotu", b + 1)
                wait(pool, "row_h", TOP * b + TOP)
                wait(pool, "row_id", b + 1)
                carry_wait()
                for k in range(TOP):
                    for c in range(C):
                        nc.gpsimd.indirect_dma_start(
                            rows_dram, bass.IndirectOffsetOnAxis(ap=SlotI[:, k, c:c + 1], axis=0), HR[:, k, c, :], None,
                            bounds_check=ROWS - 1, oob_is_err=False).then_inc(s["scat"], 16)

            pipeline(pool, p1_keys=keys, p1_outgate=outgate, p2_state=low_parts, p2_project=project, p3_rows=rows,
                     p3_scatter=scatter)

            def nothing(j, r, turn):
                return

            def c2(j, r, turn):
                wait(pool, "held", j + B)
                wait(pool, "ys", j + 1)
                carry_wait()
                for half in range(BH):
                    nc.gpsimd.indirect_dma_start(
                        y_dram, bass.IndirectOffsetOnAxis(ap=Ids[r][:, half:half + 1], axis=0), YS[r][:, half, :], None,
                        bounds_check=TOP * N - 1, oob_is_err=False).then_inc(s[f"ysc{r}"], 16)

            run_blocks(pool, block_pipeline(nothing, nothing, nothing, c2))

        @block.scalar
        def _(act):
            nc.scalar.preload_act_table_set("natural_log_exp_and_others")
            act.wait_ge(s["c_in"], 16)
            nc.scalar.activation(SC[:, 0, :], CT[:], ACT.Abs).then_inc(s["silu_act"], 1)
            act.wait_ge(s["silu_act"], 1)
            nc.scalar.activation(SC[:, 1, :], SC[:, 0, :], ACT.Exp, scale=-1.0).then_inc(s["silu_act"], 1)
            act.wait_ge(s["silu_act"], 2)
            nc.scalar.activation(SC[:, 2, :], SC[:, 1, :], ACT.Ln, bias=1.0).then_inc(s["silu_act"], 1)
            act.wait_ge(s["silu_dve"], 1)
            nc.scalar.activation(SC[:, 3, :], SC[:, 3, :], ACT.Exp).then_inc(s["silu_act"], 1)
            act.wait_ge(s["cols_ps"], 1)
            nc.scalar.activation(Cols[:, 0, :], psT[:, 0:B], ACT.Copy).then_inc(s["cols"], 1)
            nc.scalar.activation(Cols[:, 1, :], psT[:, B:2 * B], ACT.Identity, bias=1.0).then_inc(s["cols"], 1)

            def rstd(b, k, mv, lnv, out):
                wait(act, mv, C * b + C)
                nc.scalar.activation(LnV[:, k, :], MV[:, k, :, 1], ACT.Ln, bias=EpsC[:]).then_inc(s[lnv], 1)
                wait(act, lnv, b + 1)
                nc.scalar.activation(Rstd[:, k, :], LnV[:, k, :], ACT.Exp, scale=-0.5).then_inc(s[out], 1)

            def norm1(b, u):
                rstd(b, 0, "mv1", "lnv1", "rstd1")

            def norm2(b, u):
                rstd(b, 1, "mv2", "lnv2", "rstd2")

            def transpose(b, u):
                wait(act, "cols", 2)
                wait(act, "xT1", b + 1)
                nc.scalar.activation(HT[:], psT[:], ACT.Identity, scale=Cols[:, 1, bass.ds(b, 1)],
                                     bias=Cols[:, 0, bass.ds(b, 1)]).then_inc(s["hT"], 1)

            def query(b, u):
                wait(act, "uT_ps", b + 1)
                nc.scalar.copy(UT[:], pjA[0:LR, :]).then_inc(s["uT"], 1)
                wait(act, "q_ps", b + 1)
                wait(act, "qs", b)
                nc.scalar.mul(Q[:], pjB[:], float(HK ** -0.5)).then_inc(s["q_sb"], 1)

            def gates(b, u):
                wait(act, "gl_ps", b + 1)
                wait(act, "cum", b)
                nc.scalar.activation(GL[:], pjA[:], ACT.Identity, bias=Gb[:]).then_inc(s["gl_sb"], 1)
                wait(act, "k_ps", b + 1)
                wait(act, "ktil", (NS + 1) * b)
                nc.scalar.copy(K[:], pjB[:].rearrange("p (c t) -> p c t", c=C)).then_inc(s["k_sb"], 1)
                wait(act, "gl_sb", b + 1)
                nc.scalar.activation(Ln1[:], GL[:], ACT.Abs).then_inc(s["abs1"], 1)
                wait(act, "abs1", b + 1)
                nc.scalar.activation(Ln1[:], Ln1[:], ACT.Exp, scale=-1.0).then_inc(s["ex1"], 1)
                wait(act, "ex1", b + 1)
                nc.scalar.activation(Ln1[:], Ln1[:], ACT.Ln, bias=1.0).then_inc(s["ln1"], 1)

            def values(b, u):
                wait(act, "o_ps", C * b)
                wait(act, "ogat", b)
                for c in range(C):
                    wait(act, "vg_ps", C * b + c + 1)
                    nc.scalar.copy(VG[:, c, :], (pjA, pjB)[c % 2][:]).then_inc(s["vg"], 1)

            def differences(b, u):
                for i in range(NS):
                    wait(act, "difk", NS * b + i + 1)
                    k = KT[:, :, i, 0:SUB * (i + 1)]
                    nc.scalar.activation(k, k, ACT.Exp, scale=1.0 / GATE_NORM).then_inc(s["expk"], 1)
                for k in range(2):
                    wait(act, "difq", 2 * b + k + 1)
                    nc.scalar.activation(ExpQ[:, k, :], ExpQ[:, k, :], ACT.Exp, scale=1.0 / GATE_NORM).then_inc(s["expq"], 1)
                wait(act, "qs", b)
                wait(act, "s_st", 3 * b)
                nc.scalar.activation(Decay[:], Cum[:, :, NS - 1, SUB - 1], ACT.Exp, scale=1.0 / GATE_NORM).then_inc(s["decay"], 1)
                nc.scalar.activation(ExpB[:], Cum[:], ACT.Exp, scale=1.0 / GATE_NORM).then_inc(s["expb"], 1)

            def keys(b, u):
                wait(act, "qe", b + 1)
                wait(act, "sc_ps", C * b)
                for h in range(H):
                    nc.scalar.activation(QB[:, h, :], QE[:], ACT.Copy, scale=HeadMask[:, h, 0:1]).then_inc(s["qblk"], 1)

            def outgate(b, u):
                wait(act, "vg", C * b + C)
                wait(act, "gate", b)
                nc.scalar.activation(AbsG[:], Gate, ACT.Abs).then_inc(s["absg"], 1)
                wait(act, "absg", b + 1)
                nc.scalar.activation(AbsG[:], AbsG[:], ACT.Exp, scale=-1.0).then_inc(s["exg"], 1)
                wait(act, "exg", b + 1)
                nc.scalar.activation(AbsG[:], AbsG[:], ACT.Ln, bias=1.0).then_inc(s["lng"], 1)
                wait(act, "ming", b + 1)
                nc.scalar.activation(AbsG[:], AbsG[:], ACT.Exp).then_inc(s["sigg"], 1)

            def scores(b, u):
                wait(act, "ket_ps", b + 1)
                nc.scalar.copy(KEt[:], psK[:, 0:3 * P].rearrange("p (c k) -> p c k", c=3)).then_inc(s["ket"], 1)
                wait(act, "rows_ps", b + 1)
                wait(act, "h2", 2 * b - 2)
                nc.scalar.copy(Rows[u][:], psT[:].rearrange("p (j d) -> p j d", j=4)).then_inc(s["rows"], 1)

            def state(b, u):
                wait(act, "stage", b * 32 + 32)
                nc.scalar.copy(W1hi[:, b, :], Stage[:, 0, :]).then_inc(s["w_hi"], 1)
                nc.scalar.copy(W2hi[:, b, :], Stage[:, 1, :]).then_inc(s["w_hi"], 1)

            def output(b, u):
                for half in range(2):
                    wait(act, "o_ps", C * b + 2 * half + 2)
                    nc.scalar.copy(O[:, 2 * half:2 * half + 2, :],
                                   psO[:].rearrange("p (c v) -> p c v", c=2)).then_inc(s["o_sb"], 1)
                wait(act, "o_sb", 2 * b + 2)
                wait(act, "at_ps", b)
                nc.scalar.activation(Sq, O[:], ACT.Square).then_inc(s["sq"], 1)

            def rms(b, u):
                wait(act, "rows_fin", b + 1)
                nc.scalar.copy(GBr[:, b, :], Rows[u][:, 3, :]).then_inc(s["gb_row"], 1)
                wait(act, "ms", b + 1)
                nc.scalar.activation(Ms[:, 1, :], Ms[:, 0, :], ACT.Ln, scale=1.0 / HV, bias=EpsC[:]).then_inc(s["lnms"], 1)
                wait(act, "lnms", b + 1)
                nc.scalar.activation(Ms[:, 1, :], Ms[:, 1, :], ACT.Exp, scale=-0.5).then_inc(s["rms"], 1)

            def output_transpose(b, u):
                for j in range(2):
                    wait(act, "oT_ps", 2 * b + j + 1)
                    nc.scalar.copy(OT[:, j, :], (psS0, psS1)[j][:]).then_inc(s["oT"], 1)

            def logits(b, u):
                wait(act, "xT2", b + 1)
                nc.scalar.copy(H2T[:], psT[:]).then_inc(s["h2T"], 1)

            def rank(b, u):
                wait(act, "sh", b + 1)
                nc.scalar.activation(Sm[:, 1, :, :], Sm[:, 0, :, :], ACT.Exp).then_inc(s["ex"], 1)

            pipeline(act, p1_norm=norm1, p3_norm=norm2, p1_transpose=transpose, p1_query=query, p1_gates=gates,
                     p1_values=values, p1_differences=differences, p1_keys=keys, p1_outgate=outgate, p2_scores=scores,
                     p2_state=state, p2_output=output, p2_rms=rms, p2_transpose=output_transpose, p3_logits=logits,
                     p3_rank=rank)

            def nothing(j, r, turn):
                return

            def b(j, r, turn):
                for half in range(BH):
                    wait(act, "h_ps", j * BH + (half + 1))
                    if half == 0:
                        wait(act, "gt_ps", j * BH - BH)
                    nc.scalar.activation(G[r % 2][:, half, :], psH[r % 2][half][:], ACT.Gelu).then_inc(s["gelu"], 1)

            def c1(j, r, turn):
                wait(act, "y_ps", j - 1 if isinstance(j, int) else j)
                for half in range(BH):
                    wait(act, "gt_ps", j * BH + (half + 1))
                    nc.scalar.copy(GThi[r % 2][:, half, :, :], psG[half][:].rearrange("p (k t) -> p k t", k=KH)).then_inc(s["gt_hi"], 1)

            run_blocks(act, block_pipeline(nothing, b, c1, nothing))
            for b in range(B):
                act.wait_ge(s[f"y_in{b}"], 32)
                for c in range(C):
                    nc.scalar.activation(Y[:, b, 0, c, :], Y[:, b, 0, c, :], ACT.Copy, scale=W01[:, b, 0, c:c + 1]).then_inc(s["yw0"], 1)

        @block.vector
        def _(dve):
            v = nc.vector
            dve.wait_ge(s["silu_act"], 3)
            v.scalar_tensor_tensor(SC[:, 3, :], CT[:], 0.0, SC[:, 2, :], ALU.min, ALU.subtract).then_inc(s["silu_dve"], 1)
            dve.wait_ge(s["silu_act"], 4)
            v.tensor_tensor(SilC[:], CT[:], SC[:, 3, :], ALU.mult).then_inc(s["silu_dve"], 1)
            dve.wait_ge(s["silu_dve"], 2)
            dve.wait_ge(s["attn_in"], 64)
            v.tensor_scalar(Wo[:], WoR, RmsW[:], None, ALU.mult).then_inc(s["wo_fin"], 1)
            v.memset(HeadMask[:], 0.0).then_inc(s["hmask"], 1)
            dve.wait_ge(s["hmask"], 1)
            for h in range(H):
                v.memset(HeadMask[h * HK:(h + 1) * HK, h, :], 1.0).then_inc(s["hmask"], 1)
            dve.wait_ge(s["hmask"], 1 + H)
            dve.wait_ge(s["const"], 11)

            def norm(b, k, src, out, names):
                bn, mv, rs, done = names
                for c in range(C):
                    v.bn_stats(St6[:, k, c, :], src[:, c, :]).then_inc(s[bn], 1)
                wait(dve, bn, C * b + C)
                v.memset(Pad[:], 0.0)
                for c in range(C):
                    v.bn_aggr(MV[:, k, c, :], St6[:, k, c, :]).then_inc(s[mv], 1)
                wait(dve, rs, b + 1)
                for c in range(C):
                    v.tensor_scalar(out[:, c, :], src[:, c, :], MV[:, k, c, 0:1], Rstd[:, k, c:c + 1],
                                    ALU.subtract, ALU.mult).then_inc(s[done], 1)

            def norm1(b, u):
                dve.wait_ge(s[f"xin{b}" if isinstance(b, int) and b < 2 else "xin2"], 16)
                wait(dve, "xT1", b)
                norm(b, 0, X[:, b, :, :], Xh, ("bn1", "mv1", "rstd1", "xhat1"))

            def norm2(b, u):
                wait(dve, "x2", b + 1)
                wait(dve, "xT2", b)
                wait(dve, "row_h", TOP * b)
                norm(b, 1, X[:, b, :, :], H2, ("bn2", "mv2", "rstd2", "xhat2"))

            def values(b, u):
                wait(dve, "ln1", b + 1)
                v.scalar_tensor_tensor(GL[:], GL[:], 0.0, Ln1[:], ALU.min, ALU.subtract).then_inc(s["g16"], 1)
                wait(dve, "g16", b + 1)
                wait(dve, "expb", b)
                v.tensor_tensor_scan(Cum[:].rearrange("p c i s -> p (c i s)"), Restart[:].rearrange("p c t -> p (c t)"),
                                     GL[:], 0.0, ALU.mult, ALU.add).then_inc(s["cum"], 1)

            def differences(b, u):
                wait(dve, "cum", b + 1)
                wait(dve, "sc_ps", C * b)
                for i in range(NS):
                    ref = Cum[:, :, i, SUB // 2 - 1:SUB // 2].to_broadcast([P, C, SUB * (i + 1)])
                    v.tensor_tensor(KT[:, :, i, 0:SUB * (i + 1)], ref,
                                    Cum[:, :, 0:i + 1, :].rearrange("p c i s -> p c (i s)"), ALU.subtract).then_inc(s["difk"], 1)
                wait(dve, "qe", b)
                wait(dve, "ktil", (NS + 1) * b)
                v.tensor_tensor(ExpQ[:, 0, :].rearrange("p (c i s) -> p (c i) s", c=C, i=NS), Cum[:].rearrange("p c i s -> p (c i) s"),
                                Cum[:, :, :, SUB // 2 - 1:SUB // 2].rearrange("p c i s -> p (c i) s").to_broadcast([P, C * NS, SUB]),
                                ALU.subtract).then_inc(s["difq"], 1)
                v.tensor_tensor(ExpQ[:, 1, :].rearrange("p (c t) -> p c t", c=C),
                                Cum[:, :, NS - 1, SUB - 1:SUB].to_broadcast([P, C, P]),
                                Cum[:].rearrange("p c i s -> p c (i s)"), ALU.subtract).then_inc(s["difq"], 1)

            def keys(b, u):
                wait(dve, "k_sb", b + 1)
                for i in range(NS):
                    wait(dve, "expk", NS * b + i + 1)
                    k = KT[:, :, i, 0:SUB * (i + 1)]
                    v.tensor_tensor(k, k, K[:, :, 0:SUB * (i + 1)], ALU.mult).then_inc(s["ktil"], 1)
                wait(dve, "expq", 2 * b + 2)
                wait(dve, "ket_ps", b)
                v.tensor_tensor(KE[:], K[:], ExpQ[:, 1, :].rearrange("p (c t) -> p c t", c=C), ALU.mult).then_inc(s["ktil"], 1)

            def outgate(b, u):
                wait(dve, "lng", b + 1)
                v.scalar_tensor_tensor(AbsG[:], Gate, 0.0, AbsG[:], ALU.min, ALU.subtract).then_inc(s["ming"], 1)

            hm = HeadMask[:].rearrange("p h v -> p (h v)")
            cm = Causal[:].rearrange("p (o t) -> p o t", o=1).to_broadcast([P, H, P])

            def masked(b, c):
                wait(dve, "sc_ps", C * b + c + 1)
                if c >= 2:
                    wait(dve, "o_ps", C * b + c - 1)
                v.tensor_tensor(PT[c % 2][:], (psS0, psS1)[c % 2][:].rearrange("p (h t) -> p h t", h=H), cm,
                                ALU.mult).then_inc(s["pt"], 1)

            def scores(b, u):
                wait(dve, "rows_ps", b)
                v.tensor_copy(SilB[:], SilC[:, bass.ds(b, 1)].to_broadcast([P, P])).then_inc(s["silu_b"], 1)
                masked(b, 0)
                masked(b, 1)

            def state(b, u):
                wait(dve, "ds_ps", b + 1)
                v.tensor_tensor(S[0][:], psD[:, 0:DV], hm, ALU.mult).then_inc(s["s_st"], 1)
                wait(dve, "rows_used", b)
                for c in (1, 2):
                    v.tensor_tensor(Stmp[:, c - 1, :], psD[:, DV:2 * DV] if c == 1 else psK[:, 0:DV], hm,
                                    ALU.mult).then_inc(s["s_tmp"], 1)
                for c in (1, 2):
                    wait(dve, "s_tmp", 2 * b + c)
                    wait(dve, "s_st", 3 * b + c)
                    v.scalar_tensor_tensor(S[c][:], S[c - 1][:], Decay[:, c:c + 1], Stmp[:, c - 1, :],
                                           ALU.mult, ALU.add).then_inc(s["s_st"], 1)

            def output(b, u):
                wait(dve, "rows", b + 1)
                wait(dve, "s_st", 3 * b + 3)
                gates, sg, ab = Rows[u][:, 0:4:3, :], Sgn[:, 0:2, :], Sgn[:, 2:4, :]
                v.tensor_scalar(sg, gates, 0.0, 2.0, ALU.is_ge, ALU.mult).then_inc(s["rows_ab"], 1)
                v.tensor_scalar(ab, gates, -1.0, None, ALU.mult).then_inc(s["rows_ab"], 1)
                wait(dve, "rows_ab", 2 * b + 2)
                v.scalar_tensor_tensor(ab, gates, 0.25, ab, ALU.max, ALU.max).then_inc(s["rows_mul"], 1)
                masked(b, 2)
                masked(b, 3)
                wait(dve, "rows_mul", b + 1)
                v.scalar_tensor_tensor(gates, sg, -1.0, ab, ALU.add, ALU.mult).then_inc(s["rows_used"], 1)
                v.tensor_scalar(Rows[u][:, 2, :], Rows[u][:, 2, :], 1.0, None, ALU.add).then_inc(s["rows_fin"], 1)

            def rms(b, u):
                wait(dve, "sq", b + 1)
                v.tensor_reduce(Ms[:, 0, :], Sq.rearrange("p c (h v) -> p (c h) v", h=H), axis=AX.X, op=ALU.add).then_inc(s["ms"], 1)
                wait(dve, "gate", b + 1)
                v.tensor_tensor(O[:], O[:], Gate, ALU.mult).then_inc(s["ogat"], 1)
                wait(dve, "ogat", b + 1)
                wait(dve, "rms", b + 1)
                v.tensor_tensor(O[:].rearrange("p c (h v) -> p (c h) v", h=H), O[:].rearrange("p c (h v) -> p (c h) v", h=H),
                                Ms[:, 1, :].rearrange("p (n o) -> p n o", o=1).to_broadcast([P, C * H, HV]), ALU.mult).then_inc(s["onrm"], 1)

            def project(b, u):
                wait(dve, "at_ps", b + 1)
                wait(dve, "x2", b)
                wait(dve, "rows_used", b + 1)
                v.tensor_tensor(At[:], psO[:].rearrange("p (c d) -> p c d", c=C), Rows[u][:, 0:1, :].to_broadcast([P, C, D]),
                                ALU.mult).then_inc(s["at_g"], 1)

            def rows(b, u):
                wait(dve, "scat", b * (16 * TOP * C))
                v.tensor_copy(HR[:, :, :, D:RW].rearrange("p k c o -> p k (c o)").bitcast(I32), Place[:, b, :, :]).then_inc(s["row_id"], 1)

            def logits(b, u):
                wait(dve, "h2", 2 * b + 2)
                for k in range(TOP):
                    v.tensor_copy(HR[:, k, :, 0:D], H2[:]).then_inc(s["row_h"], 1)
                wait(dve, "lg_ps", b + 1)
                v.tensor_copy(LG[:], psT[:, 0:C * E].rearrange("p (c e) -> p c e", c=C)).then_inc(s["lg"], 1)

            def rank(b, u):
                wait(dve, "lg", b + 1)
                mine = LG[:].rearrange("p c (e o) -> p c e o", o=1).to_broadcast([P, C, E, E])
                other = LG[:].rearrange("p c (o e) -> p c o e", o=1).to_broadcast([P, C, E, E])
                v.tensor_tensor(Rk[:, 0, :, :, :], other, mine, ALU.is_gt).then_inc(s["rk01"], 1)
                v.tensor_tensor(Rk[:, 1, :, :, :], other, mine, ALU.is_equal).then_inc(s["rk01"], 1)
                v.tensor_reduce(R1[:, 0, :], LG[:], axis=AX.X, op=ALU.max).then_inc(s["route"], 1)
                wait(dve, "rk01", 2 * b + 2)
                bf = Before[:].rearrange("p e j -> p (e j)").rearrange("p (o n) -> p o n", o=1).to_broadcast([P, C, E * E])
                rk = [Rk[:, j, :, :, :].rearrange("p c e j -> p c (e j)") for j in range(2)]
                v.tensor_tensor(rk[1], rk[1], bf, ALU.mult).then_inc(s["route"], 1)
                wait(dve, "route", 9 * b + 1)
                v.tensor_tensor(Sm[:, 0, :, :], LG[:], R1[:, 0, :].rearrange("p (c o) -> p c o", o=1).to_broadcast([P, C, E]),
                                ALU.subtract).then_inc(s["sh"], 1)
                wait(dve, "route", 9 * b + 2)
                v.tensor_tensor(rk[0], rk[0], rk[1], ALU.add).then_inc(s["route"], 1)
                wait(dve, "route", 9 * b + 3)
                v.tensor_reduce(Sm[:, 2, :, :].rearrange("p c e -> p (c e)"), Rk[:, 0, :, :, :].rearrange("p c e j -> p (c e) j"),
                                axis=AX.X, op=ALU.add).then_inc(s["rk4"], 1)
                wait(dve, "rk4", b + 1)
                rank = Sm[:, 2, :, :]
                v.tensor_scalar(Sel[:], rank, TOP - 0.5, None, ALU.is_lt).then_inc(s["sel"], 1)
                for k in range(TOP):
                    v.tensor_scalar(Sel2[:, k, :, :], rank, float(k), None, ALU.is_equal).then_inc(s["sel2"], 1)
                wait(dve, "count", b * C)
                wait(dve, "pos_ps", b)
                v.tensor_copy(Count[:, 0, :], Count[:, C, :]).then_inc(s["carry"], 1)
                wait(dve, "carry", b + 1)
                wait(dve, "sel", b + 1)
                for c in range(C):
                    wait(dve, "count", b * C + c)
                    v.tensor_tensor(Count[:, c + 1, :], Count[:, c, :], Sel[:, c, :], ALU.add).then_inc(s["count"], 1)
                wait(dve, "ex", b + 1)
                v.tensor_reduce(R1[:, 1, :], Sm[:, 1, :, :], axis=AX.X, op=ALU.add).then_inc(s["route"], 1)
                wait(dve, "route", 9 * b + 4)
                v.reciprocal(R1[:, 2, :], R1[:, 1, :]).then_inc(s["route"], 1)
                wait(dve, "route", 9 * b + 5)
                v.tensor_tensor(Sm[:, 3, :, :], Sm[:, 1, :, :], R1[:, 2, :].rearrange("p (c o) -> p c o", o=1).to_broadcast([P, C, E]),
                                ALU.mult).then_inc(s["route"], 1)
                wait(dve, "route", 9 * b + 6)
                wait(dve, "sel2", b * TOP + TOP)
                flat = lambda a: a.rearrange("p c e -> p (c e)").rearrange("p (o n) -> p o n", o=1).to_broadcast([P, TOP, C * E])
                sel2 = Sel2[:].rearrange("p k c e -> p k (c e)")
                pick = [Pick[:, j, :, :, :].rearrange("p k c e -> p k (c e)") for j in range(2)]
                pickr = [Pick[:, j, :, :, :].rearrange("p k c e -> p (k c) e") for j in range(2)]
                v.tensor_tensor(pick[0], sel2, flat(Sm[:, 3, :, :]), ALU.mult).then_inc(s["route"], 1)
                wait(dve, "route", 9 * b + 7)
                v.tensor_reduce(W01[:, b, :, :].rearrange("p k c -> p (k c)"), pickr[0], axis=AX.X, op=ALU.add).then_inc(s["w01"], 1)

            def slots(b, u):
                flat = lambda a: a.rearrange("p c e -> p (c e)").rearrange("p (o n) -> p o n", o=1).to_broadcast([P, TOP, C * E])
                sel2 = Sel2[:].rearrange("p k c e -> p k (c e)")
                pick = [Pick[:, j, :, :, :].rearrange("p k c e -> p k (c e)") for j in range(2)]
                pickr = [Pick[:, j, :, :, :].rearrange("p k c e -> p (k c) e") for j in range(2)]
                wait(dve, "pos_ps", b + 1)
                v.tensor_tensor(Sm[:, 0, :, :], psT[:, 2 * C * E:3 * C * E].rearrange("p (c e) -> p c e", c=C),
                                RegE[:].rearrange("p (o e) -> p o e", o=1).to_broadcast([P, C, E]), ALU.add).then_inc(s["slot"], 1)
                wait(dve, "slot", b + 1)
                v.tensor_tensor(pick[1], sel2, flat(Sm[:, 0, :, :]), ALU.mult).then_inc(s["route"], 1)
                wait(dve, "route", 9 * b + 8)
                v.tensor_reduce(Slot[:].rearrange("p k c -> p (k c)"), pickr[1], axis=AX.X, op=ALU.add).then_inc(s["route"], 1)
                wait(dve, "route", 9 * b + 9)
                v.tensor_copy(SlotI[:], Slot[:]).then_inc(s["slotu"], 1)


            pipeline(dve, p1_norm=norm1, p3_norm=norm2, p1_values=values, p1_differences=differences, p1_keys=keys,
                     p1_outgate=outgate, p2_scores=scores, p2_state=state, p2_output=output, p2_rms=rms,
                     p2_project=project, p3_rows=rows, p3_logits=logits, p3_rank=rank, p3_slots=slots)

            chain = [0]

            def link(ins):
                chain[0] += 1
                ins.then_inc(s["table"], 1)
                dve.wait_ge(s["table"], chain[0])

            dve.wait_ge(s["cnt_ps"], 1)
            dve.wait_ge(s["w_lo"], TOP * E)
            link(v.tensor_copy(Nb[:, 0, :], psT[:, 0:E]))
            v.tensor_tensor(PadAt[:], Nb[:, 0, :], RegE[:], ALU.add).then_inc(s["pad_at"], 1)
            link(v.tensor_scalar(NbI[:, 0, :], Nb[:, 0, :], float(BT - 1), None, ALU.add))
            link(v.tensor_scalar(NbI[:, 1, :], NbI[:, 0, :], BT.bit_length() - 1, None, ALU.logical_shift_right))
            link(v.tensor_copy(Nb[:, 1, :], NbI[:, 1, :]))
            link(v.tensor_tensor_scan(Nb[:, 2, :], Ones[:, 0:E], Nb[:, 1, :], 0.0, ALU.mult, ALU.add))
            ends = Nb[:, 2, :].rearrange("p (o e) -> p o e", o=1).to_broadcast([P, NBLK, E])
            jn = Jn[:].rearrange("p (j o) -> p j o", o=1).to_broadcast([P, NBLK, E])
            link(v.tensor_tensor(Le[:, 0, :, :], ends, jn, ALU.is_le))
            link(v.tensor_reduce(Bl[:, 0, :], Le[:, 0, :, :], axis=AX.X, op=ALU.add))
            v.tensor_scalar(Tab[:, 1, :], Bl[:, 0, :], float(E - 1), None, ALU.min).then_inc(s["tab_e"], 1)
            link(v.tensor_tensor(Le[:, 1, :, :], Le[:, 0, :, :], Nb[:, 1, :].rearrange("p (o e) -> p o e", o=1).to_broadcast([P, NBLK, E]), ALU.mult))
            link(v.tensor_reduce(Bl[:, 1, :], Le[:, 1, :, :], axis=AX.X, op=ALU.add))
            link(v.tensor_tensor(Bl[:, 2, :], Jn[:], Bl[:, 1, :], ALU.subtract))
            link(v.tensor_scalar(Bl[:, 3, :], Bl[:, 0, :], float(REG), None, ALU.mult))
            link(v.scalar_tensor_tensor(Bl[:, 0, :], Bl[:, 2, :], float(BT), Bl[:, 3, :], ALU.mult, ALU.add))
            v.tensor_scalar(Tab[:, 0, :], Bl[:, 0, :], float(SPARE), None, ALU.min).then_inc(s["tab_row"], 1)

            def a(j, r, turn):
                wait(dve, "xt_ps", j + 1)
                wait(dve, "h_ps", j * BH - BH)
                v.tensor_copy(XThi[r % 2][:], psX[:, 0:BT]).then_inc(s["xt_hi"], 1)
                wait(dve, f"ysc{r}", turn * (16 * BH))
                v.tensor_copy(Ids[r][:], XR[r][:, :, D].bitcast(U32)).then_inc(s["ids"], 1)
                wait(dve, "xt_hi", j + 1)
                v.tensor_tensor(XTlo[r % 2][:], psX[:, 0:BT], XThi[r % 2][:].bitcast(F32), ALU.subtract).then_inc(s["xt_lo"], 1)

            def nothing(j, r, turn):
                return

            def c1(j, r, turn):
                for half in range(BH):
                    wait(dve, "gt_hi", j * BH + (half + 1))
                    v.tensor_tensor(GTlo[r % 2][:, half, :, :], psG[half][:].rearrange("p (k t) -> p k t", k=KH),
                                    GThi[r % 2][:, half, :, :].bitcast(F32), ALU.subtract).then_inc(s["gt_lo"], 1)

            def c2(j, r, turn):
                wait(dve, "y_ps", j + 1)
                v.tensor_copy(YS[r][:], psY[:, 0:BH * D].rearrange("p (h d) -> p h d", h=BH)).then_inc(s["ys"], 1)

            run_blocks(dve, block_pipeline(a, nothing, c1, c2))
            dve.wait_ge(s["w01"], B)
            dve.wait_ge(s["gb_row"], B)
            for b in range(B):
                dve.wait_ge(s[f"y_in{b}"], 32)
                for c in range(C):
                    dve.wait_ge(s["yw0"], b * C + c + 1)
                    v.scalar_tensor_tensor(Y[:, b, 1, c, :], Y[:, b, 1, c, :], W01[:, b, 1, c:c + 1], Y[:, b, 0, c, :],
                                           ALU.mult, ALU.add).then_inc(s["yw"], 1)
                dve.wait_ge(s["yw"], (b + 1) * C)
                v.tensor_tensor(Y[:, b, 1, :, :], Y[:, b, 1, :, :], GBr[:, b:b + 1, :].to_broadcast([P, C, D]), ALU.mult).then_inc(s["ygb"], 1)
                dve.wait_ge(s["ygb"], b + 1)
                v.tensor_tensor(X[:, b, :, :], Y[:, b, 1, :, :], X[:, b, :, :], ALU.add).then_inc(s["yfin"], 1)

        @block.tensor
        def _(pe):
            mm = nc.tensor.matmul
            pe.wait_ge(s["wmod_in"], 16)
            pe.wait_ge(s["silu_dve"], 2)
            for j in range(2):
                ins = mm(psT[:, j * B:(j + 1) * B], Wmod[:, j * D:(j + 1) * D], SilC[:], start=True, stop=True)
            ins.then_inc(s["cols_ps"], 1)
            pe.wait_ge(s["ident"], 1)
            pe.wait_ge(s["proj_in"], 96)
            pe.wait_ge(s["cols"], 2)

            def transpose(b, u):
                wait(pe, "xhat1", C * b + C)
                wait(pe, "rows", b)
                for c in range(C):
                    ins = nc.tensor.transpose(psT[:, c * P:(c + 1) * P], Xh[:, c, :], Id[:])
                ins.then_inc(s["xT1"], 1)

            def query(b, u):
                wait(pe, "hT", b + 1)
                wait(pe, "vg", C * b)
                mm(pjA[0:LR, :], W1k[:], HT[:], start=True, stop=True).then_inc(s["uT_ps"], 1)
                mm(pjB[:], Wq[:], HT[:], start=True, stop=True).then_inc(s["q_ps"], 1)

            def gates(b, u):
                wait(pe, "uT", b + 1)
                mm(pjA[:], W2k[:], UT[:], start=True, stop=True).then_inc(s["gl_ps"], 1)
                wait(pe, "q_sb", b + 1)
                mm(pjB[:], Wk[:], HT[:], start=True, stop=True).then_inc(s["k_ps"], 1)

            def values(b, u):
                for c in range(C):
                    if c == 0:
                        wait(pe, "gl_sb", b + 1)
                    elif c == 1:
                        wait(pe, "k_sb", b + 1)
                    else:
                        wait(pe, "vg", C * b + c - 1)
                    mm((pjA, pjB)[c % 2][:], HT[:, c * P:(c + 1) * P], Wvg[:], start=True, stop=True).then_inc(s["vg_ps"], 1)

            def score(b, c):
                if c >= 2:
                    wait(pe, "pt", C * b + c - 1)
                ps = (psS0, psS1)[c % 2][:].rearrange("p (h i t) -> p h i t", h=H, i=NS)
                for i in range(NS):
                    t0 = c * P + i * SUB
                    ins = mm(ps[:, :, i, :], KT[:, c, i, :], QB[:, :, t0:t0 + SUB], start=True, stop=True)
                ins.then_inc(s["sc_ps"], 1)

            def chunk(b, c):
                o = psO[:, (c % 2) * DV:(c % 2 + 1) * DV]
                wait(pe, "pt", C * b + c + 1)
                if c:
                    wait(pe, "s_st", 3 * b + c)
                    mm(o, QS[:, c * P:(c + 1) * P], S[c - 1][:], start=True, stop=False, skip_group_check=True)
                for h in range(H):
                    ins = mm(o[:, h * HV:(h + 1) * HV], PT[c % 2][:, h, :], VG[:, c, h * HV:(h + 1) * HV],
                             start=(c == 0), stop=(c == 0 or h == H - 1), skip_group_check=True)
                ins.then_inc(s["o_ps"], 1)

            def scores(b, u):
                wait(pe, "ktil", (NS + 1) * b + NS + 1)
                wait(pe, "s_tmp", 2 * b)
                for c in range(3):
                    ins = nc.tensor.transpose(psK[:, c * P:(c + 1) * P], KE[:, c, :], Id[:])
                ins.then_inc(s["ket_ps"], 1)
                wait(pe, "qblk", H * b + H)
                wait(pe, "oT", 2 * b)
                score(b, 0)
                score(b, 1)
                wait(pe, "silu_b", b + 1)
                wait(pe, "slot", b - 1)
                mm(psT[:], SilB[:], Wmod[:, 2 * D:6 * D], start=True, stop=True).then_inc(s["rows_ps"], 1)

            def state(b, u):
                wait(pe, "ket", b + 1)
                wait(pe, "vg", C * b + C)
                for c in range(3):
                    ds = psD[:, c * DV:(c + 1) * DV] if c < 2 else psK[:, 0:DV]
                    ins = mm(ds, KEt[:, c, :], VG[:, c, 0:DV], start=True, stop=True)
                ins.then_inc(s["ds_ps"], 1)
                wait(pe, "qs", b + 1)
                wait(pe, "at_g", b)
                chunk(b, 0)
                chunk(b, 1)

            def output(b, u):
                score(b, 2)
                score(b, 3)
                wait(pe, "o_sb", 2 * b + 1)
                chunk(b, 2)
                chunk(b, 3)

            def output_transpose(b, u):
                wait(pe, "onrm", b + 1)
                wait(pe, "pt", C * b + C)
                for j, ps in enumerate((psS0, psS1)):
                    for c in range(C):
                        ins = nc.tensor.transpose(ps[:, c * P:(c + 1) * P], O[:, c, j * P:(j + 1) * P], Id[:])
                    ins.then_inc(s["oT_ps"], 1)

            def project(b, u):
                wait(pe, "wo_fin", 1)
                wait(pe, "oT", 2 * b + 2)
                wait(pe, "o_sb", 2 * b + 2)
                for c in range(C):
                    for j in range(2):
                        ins = mm(psO[:, c * P:(c + 1) * P], OT[:, j, c * P:(c + 1) * P], Wo[:, j, :],
                                 start=(j == 0), stop=(j == 1))
                ins.then_inc(s["at_ps"], 1)

            def logits(b, u):
                wait(pe, "h2", 2 * b + 2)
                if not isinstance(b, int) or b < B - 2:
                    wait(pe, "hT", b + 3)
                wait(pe, "rows", b + 2 if not isinstance(b, int) or b < B - 1 else B)
                for c in range(C):
                    ins = nc.tensor.transpose(psT[:, c * P:(c + 1) * P], H2[:, c, :], Id[:])
                ins.then_inc(s["xT2"], 1)
                wait(pe, "h2T", b + 1)
                wait(pe, "attn_in", 64)
                for c in range(C):
                    ins = mm(psT[:, c * E:(c + 1) * E], H2T[:, c * P:(c + 1) * P], Rw[:], start=True, stop=True)
                ins.then_inc(s["lg_ps"], 1)

            def rank(b, u):
                wait(pe, "lg", b + 1)
                wait(pe, "count", b * C + C)
                pos = psT[:, 2 * C * E:3 * C * E]
                mm(pos, Earlier[:], Sel[:].rearrange("p c e -> p (c e)"), start=True, stop=False)
                mm(pos, Ones[:], Count[:, 0:C, :].rearrange("p c e -> p (c e)"), start=False, stop=True).then_inc(s["pos_ps"], 1)

            pipeline(pe, p1_transpose=transpose, p1_query=query, p1_gates=gates, p1_values=values, p2_scores=scores,
                     p2_state=state, p2_output=output, p2_transpose=output_transpose, p2_project=project,
                     p3_logits=logits, p3_rank=rank)

            pe.wait_ge(s["slot"], B)
            mm(psT[:, 0:E], Ones[:], Count[:, C, :], start=True, stop=True).then_inc(s["cnt_ps"], 1)
            pe.wait_ge(s["tab_e"], 1)
            pe.wait_ge(s["w_lo"], TOP * E)
            pe.wait_ge(s["at_g"], B)

            def three(out_, hi, lo, whi, wlo, start, stop):
                mm(out_, hi, whi, start=start, stop=False)
                mm(out_, hi, wlo, start=False, stop=False)
                return mm(out_, lo, whi, start=False, stop=stop)

            def expert(j):
                at = Tab[0:1, 1, j:j + 1] if isinstance(j, int) else Tab[0:1, 1, bass.ds(j, 1)]
                return pe.value_load(at, min_val=0, max_val=E - 1)

            def a(j, r, turn):
                wait(pe, f"xblk{r}", turn * 16 + 16)
                wait(pe, "xt_lo", j)
                for half in range(BH):
                    ins = nc.tensor.transpose(psX[:, half * P:(half + 1) * P], XR[r][:, half, 0:D], Id[:])
                ins.then_inc(s["xt_ps"], 1)

            def b(j, r, turn):
                e = expert(j)
                wait(pe, "xt_lo", j + 1)
                wait(pe, "gelu", (j - 1) * BH)
                for half in range(BH):
                    t = slice(half * P, (half + 1) * P)
                    three(psH[r % 2][half][:], XThi[r % 2][:, t], XTlo[r % 2][:, t], W1hi[:, bass.ds(e, 1), :].rearrange("p o n -> p (o n)"),
                          W1lo[:, bass.ds(e, 1), :].rearrange("p o n -> p (o n)"), True, True).then_inc(s["h_ps"], 1)

            def c1(j, r, turn):
                wait(pe, "gt_lo", j * BH)
                for half in range(BH):
                    wait(pe, "gelu", j * BH + (half + 1))
                    for k in range(KH):
                        ins = nc.tensor.transpose(psG[half][:, k * P:(k + 1) * P], G[r % 2][:, half, k * P:(k + 1) * P], Id[:])
                    ins.then_inc(s["gt_ps"], 1)

            def c2(j, r, turn):
                e = expert(j)
                wait(pe, "ys", j)
                for half in range(BH):
                    wait(pe, "gt_lo", j * BH + (half + 1))
                    for k in range(KH):
                        w2 = [w[:, bass.ds(e, 1), k * D:(k + 1) * D].rearrange("p o n -> p (o n)") for w in (W2hi, W2lo)]
                        ins = three(psY[:, half * D:(half + 1) * D], GThi[r % 2][:, half, k, :], GTlo[r % 2][:, half, k, :],
                                    w2[0], w2[1], k == 0, k == KH - 1)
                ins.then_inc(s["y_ps"], 1)

            run_blocks(pe, block_pipeline(a, b, c1, c2))


_INS = ["x", "cT", "wmod", "wq", "wk", "wvg", "gk_w1", "gk_w2", "gk_b", "wo", "rms_w", "rwT", "w1T", "w2T"]


def kernel(**inputs):
    import concourse.bacc as bacc
    from concourse.bass_utils import run_bass_kernel_spmd

    i = {k.removeprefix("L0_"): np.asarray(v) for k, v in inputs.items()}
    laid = {
        "x": i["attn_x"],
        "cT": i["c"].T,
        "wmod": i["wmod"],
        "wq": i["attn_Wq"],
        "wk": i["attn_Wk"],
        "wvg": np.concatenate([i["attn_Wv"], i["attn_Wg"]], axis=1),
        "gk_w1": i["attn_gk_w1"],
        "gk_w2": i["attn_gk_w2"],
        "gk_b": i["attn_gk_b"].reshape(DK, 1),
        "wo": i["attn_Wo"].reshape(2, P, D).transpose(1, 0, 2),
        "rms_w": i["attn_rms_w"].reshape(HV, 1),
        "rwT": i["ffn_router_w"].T,
        "w1T": i["ffn_w1"].transpose(2, 0, 1),
        "w2T": i["ffn_w2"].reshape(E, D, KH, P).transpose(3, 0, 2, 1).reshape(P, E, HID),
    }
    nc = bacc.Bacc("TRN2", target_bir_lowering=False, num_devices=1)
    arrays, args = {}, []
    for name in _INS:
        a = np.ascontiguousarray(laid[name])
        arrays[f"in_{name}"] = a
        args.append(nc.dram_tensor(f"in_{name}", a.shape, mybir.dt.from_np(a.dtype), kind="ExternalInput").ap())
    args.append(nc.dram_tensor("out", (B, T, D), F32, kind="ExternalOutput").ap())
    build_program(nc, *args)
    r = run_bass_kernel_spmd(nc, [arrays], core_ids=[0])
    return r.results[0]["out"]
```

```python
from contextlib import ExitStack

import numpy as np

import concourse.bass as bass
from concourse import mybir

F32 = mybir.dt.float32
F32R = mybir.dt.float32r
I32, U32 = mybir.dt.int32, mybir.dt.uint32
ALU = mybir.AluOpType
ACT = mybir.ActivationFunctionType
AX = mybir.AxisListType

P = 128
B, T, D = 8, 512, 128
H, HK, HV = 4, 32, 64
DK, DV = H * HK, H * HV
LR = 16
C = T // P
SUB = 32
NS = P // SUB
E, HID = 8, 512
KH = HID // P
HB = 2
KB = KH // HB
EPS = 1e-5
GATE_NORM = 16.0
MODS = 6
N = B * T
TOP = 2
BT = 256
BH = BT // P
REG = N + BT
SPARE = E * REG
ROWS = SPARE + BT
RING = 4
NBLK = (TOP * N + E * (BT - 1)) // BT
TURNS = (NBLK - 2) // RING
POOL_OUT = (1, 5)
DVE_OUT = tuple(b for b in range(B) if b not in POOL_OUT)
START = 1
RW = D + 2


def build_program(nc, x, cT, wmod, wq, wk, wvg, gk_w1, gk_w2, gk_b, wo, rms_w, rwT, w1T, w2T, out):
    rows_dram = nc.dram_tensor("expert_rows", (ROWS, RW), F32, kind="Internal").ap()
    y_dram = nc.dram_tensor("expert_out", (TOP * N, D), F32, kind="Internal").ap()
    with ExitStack() as ctx:
        def sb(name, shape, dt=F32):
            return ctx.enter_context(nc.sbuf_tensor(name, shape, dt))

        def bank(name):
            return ctx.enter_context(nc.psum_tensor(name, [P, 512], F32))

        def sem(name):
            return ctx.enter_context(nc.semaphore(name))

        W1 = sb("W1", [P, E, 2, HID], F32R)
        W2 = sb("W2", [P, E, KH, 2, D], F32R)
        Id = sb("Id", [P, P])
        X = sb("X", [P, B, C, D])
        GBr = sb("GBr", [P, B, D])
        Count = sb("Count", [P, C + 1, E])
        PadP = sb("PadP", [P, 1])
        PadRow = sb("PadRow", [P, BH, RW])
        Tab = sb("Tab", [P, 2, NBLK], I32)
        PadAt = sb("PadAt", [P, E], I32)

        a_ctx = ExitStack()

        def sa(name, shape, dt=F32):
            return a_ctx.enter_context(nc.sbuf_tensor(name, shape, dt))

        Stage = sa("Stage", [P, 2, HID])
        Wmod = sa("Wmod", [P, MODS * D])
        CT = sa("CT", [P, B])
        Wq, Wk = sa("Wq", [P, DK]), sa("Wk", [P, DK])
        Wvg = sa("Wvg", [P, 2 * DV])
        W1k, W2k = sa("W1k", [P, LR]), sa("W2k", [LR, DK])
        Gb = sa("Gb", [P, 1])
        Wo = sa("Wo", [P, 2, D])
        RmsW = sa("RmsW", [P, 1])
        Rw = sa("Rw", [P, E])
        Causal = sa("Causal", [P, P])
        Earlier = sa("Earlier", [P, P])
        Ones = sa("Ones", [P, P])
        HeadMask = sa("HeadMask", [P, H, HV])
        Restart = sa("Restart", [P, C, P], mybir.dt.bfloat16)
        Before = sa("Before", [P, E, E])
        EpsC = sa("EpsC", [P, 1])
        Place = sa("Place", [P, B, TOP, C], I32)
        RegE = sa("RegE", [P, E])
        Jn = sa("Jn", [P, NBLK])
        SC = sa("SC", [P, 4, B])
        SilC = sa("SilC", [P, B])
        SilB = sa("SilB", [P, P])
        Cols = sa("Cols", [P, 2, B])
        Rows = [sa(f"Rows{u}", [P, 4, D]) for u in range(2)]
        St6 = sa("St6", [P, 2, C, 6])
        Pad = sa("Pad", [P, 1])
        MV = sa("MV", [P, 2, C, 2])
        LnV, Rstd = sa("LnV", [P, 2, C]), sa("Rstd", [P, 2, C])
        Xh = sa("Xh", [P, C, D])
        HT = sa("HT", [P, T])
        H2T = sa("H2T", [P, T])
        UT = sa("UT", [LR, T])
        Q, K = sa("Q", [P, T]), sa("K", [P, C, P])
        GL, Ln1 = sa("GL", [P, T]), sa("Ln1", [P, T])
        Cum = sa("Cum", [P, C, NS, SUB])
        ExpQ = sa("ExpQ", [P, 2, T])
        ExpB = sa("ExpB", [P, T])
        Decay = sa("Decay", [P, C])
        KT = sa("KT", [P, C, NS, P])
        KE = sa("KE", [P, C, P])
        QE = sa("QE", [P, T])
        WoR = QE[:, 0:2 * D].rearrange("p (j d) -> p j d", j=2)
        QB = sa("QB", [P, H, T])
        QS = sa("QS", [P, T])
        VG = sa("VG", [P, C, 2 * DV])
        AbsG = sa("AbsG", [P, C, DV])
        Gate = VG[:, :, DV:]
        KEt = sa("KEt", [P, 3, P])
        PT = [sa(f"PT{i}", [P, H, P]) for i in range(2)]
        S = [sa(f"S{c}", [P, DV]) for c in range(3)]
        Stmp = sa("Stmp", [P, 2, DV])
        Sgn = Stmp[:].rearrange("p a v -> p (a v)").rearrange("p (j d) -> p j d", j=4)
        O = sa("O", [P, C, DV])
        Ms = sa("Ms", [P, 2, C * H])
        OT = sa("OT", [P, 2, T])
        Sq = OT[:].rearrange("p j t -> p (j t)").rearrange("p (c v) -> p c v", c=C)
        At = sa("At", [P, C, D])
        H2 = sa("H2", [P, C, D])
        HR = [sa(f"HR{u}", [P, TOP, C, RW]) for u in range(2)]
        LG = sa("LG", [P, C, E])
        Rk = sa("Rk", [P, 2, C, E, E])
        Sm = sa("Sm", [P, 4, C, E])
        Sel = sa("Sel", [P, C, E])
        Sel2 = sa("Sel2", [P, TOP, C, E])
        Pick = sa("Pick", [P, 2, TOP, C, E])
        Slot = sa("Slot", [P, TOP, C])
        SlotI = [sa(f"SlotI{u}", [P, TOP, C], U32) for u in range(2)]
        R1 = sa("R1", [P, 4, C])
        Nb = sa("Nb", [P, 4, E])
        NbI = sa("NbI", [P, 2, E], I32)
        Le = Stage[:].rearrange("p a n -> p (a n)")[:, 0:2 * NBLK * E].rearrange("p (a j e) -> p a j e", a=2, e=E)
        Bl = sa("Bl", [P, 4, NBLK])
        a_ctx.close()
        XR = [sb(f"XR{r}", [P, BH, RW]) for r in range(RING)]
        Ids = [sb(f"Ids{r}", [P, BH, 2], U32) for r in range(RING)]
        W1b = [sb(f"W1b{u}", [P, 2, HID], F32R) for u in range(2)]
        XThi = [sb(f"XThi{u}", [P, BT], F32R) for u in range(2)]
        XTlo = [sb(f"XTlo{u}", [P, BT], F32R) for u in range(2)]
        G = [sb(f"G{u}", [P, KH, BT]) for u in range(2)]
        Ghi = [sb(f"Ghi{u}", [P, KH, BT], F32R) for u in range(2)]
        Glo = [sb(f"Glo{u}", [P, KH, BT], F32R) for u in range(2)]
        YS = [sb(f"YS{r}", [P, BH, D]) for r in range(RING)]
        Y = sb("Y", [P, B, TOP, C, D])

        psA = [bank(f"ps{i}") for i in range(8)]
        psT, pjA, pjB, psS0, psS1, psK, psD, psO = psA
        psX, psH, psY = (psA[0], psA[7]), (psA[1:3], psA[3:5]), psA[5:7]

        names = ("c_in wmod_in proj_in attn_in ident_a ident const silu_b cols_ps cols rows_ps rows rows_used rows_mul "
                 "rows_fin wo_fin bn1 mv1 lnv1 rstd1 xhat1 xT1 hT uT_ps uT q_ps q_sb gl_ps gl_sb k_ps k_sb vg_ps abs1 "
                 "ex1 ln1 g16 cum difk difq expk expq expb ktil qe hmask qblk qs absg exg lng ming sigg gate ket_ps "
                 "ket sc_ps pt ds_ps s_tmp s_st o_ps o_sb sq ms lnms rms onrm ogat at_ps at_g x2 bn2 mv2 lnv2 rstd2 "
                 "xhat2 h2 xT2 h2T lg_ps lg row_h row_id rk4 sh ex sel sel2 carry count pos_ps slot w01 slotu scat0 scat1 "
                 "stage w_hi w_lo cnt_ps tab_row tab_e pad_at padrow pads table gb_row decay xt_ps xt_hi xt_lo h_ps "
                 "gelu w1_b g_hi g_lo y_ps yhi ys0 ys1 ysum ygb yfin ysum_p ygb_p yfin_p out_dma silu_act silu_dve rk01 rows_ab oT_ps held "
                 "xin0 xin1 route ids xblk0 xblk1 xblk2 xblk3 ysc0 ysc1 ysc2 ysc3 xin2 vg oT ").split()
        names += [f"y_in{b}" for b in range(B)]
        s = {n: sem(n) for n in names}

        def wait(eng, name, value):
            if isinstance(value, int) and value <= 0:
                return
            eng.wait_ge(s[name], value)

        block = ctx.enter_context(nc.Block())

        def last(b):
            return isinstance(b, int) and b == B - 1

        def output_gate(eng, ops, b):
            wait(eng, "o_sb", 2 * b + 2)
            wait(eng, "sq", b + 1)
            wait(eng, "gate", b + 1)
            ops.tensor_tensor(O[:], O[:], AbsG[:], ALU.mult).then_inc(s["ogat"], 1)

        def add_attention(eng, ops, b):
            wait(eng, "at_g", b + 1)
            ops.tensor_tensor(X[:, b, :, :], X[:, b, :, :], At[:], ALU.add).then_inc(s["x2"], 1)

        def modulate(eng, ops, b, u):
            wait(eng, "xhat2", b * C + C)
            wait(eng, "rows_fin", b + 1)
            ops.tensor_tensor(H2[:], H2[:], Rows[u][:, 2:3, :].to_broadcast([P, C, D]), ALU.mult).then_inc(s["h2"], 1)
            wait(eng, "h2", 2 * b + 1)
            ops.tensor_tensor(H2[:], H2[:], Rows[u][:, 1:2, :].to_broadcast([P, C, D]), ALU.add).then_inc(s["h2"], 1)

        def part(piece, which):
            return lambda b, u: piece(b, u, which)

        def pipeline(eng, order, **piece):
            steps = [(word[:-2], int(word[-2:])) for word in order.split()]
            assert sorted(n for n, k in steps) == sorted(piece)
            ahead, behind = max(k for n, k in steps), -min(k for n, k in steps)

            def turn(t, parity):
                for name, k in steps:
                    if not isinstance(t, int) or 0 <= t + k < B:
                        piece[name](t + k, (parity + k) % 2)

            first = max(behind + START, 2 - ahead)
            pairs = (B - 1 - ahead - first) // 2
            for t in range(-ahead, first):
                turn(t, t % 2)
            with eng.Fori(0, pairs) as i:
                for j in range(2):
                    turn(i * 2 + (first + j), (first + j) % 2)
            for t in range(first + 2 * pairs, B + behind):
                turn(t, t % 2)

        def block_pipeline(a, b, c):
            def step(j, r, turn, rest):
                if rest >= 2:
                    a(j + 2, (r + 2) % RING, turn + (r + 2) // RING)
                if rest >= 1:
                    b(j + 1, (r + 1) % RING, turn + (r + 1) // RING)
                c(j, r, turn)

            a(0, 0, 0)
            a(1, 1, 0)
            b(0, 0, 0)
            return step

        def run_blocks(eng, step):
            with eng.Fori(0, TURNS) as i:
                for r in range(RING):
                    step(i * RING + r, r, i, 2)
            for j in range(TURNS * RING, NBLK):
                step(j, j % RING, j // RING, NBLK - 1 - j)

        def nothing(j, r, turn):
            pass

        def result(eng, ops, b, n, names):
            added, scaled, done = names
            eng.wait_ge(s[f"y_in{b}"], 16 * TOP)
            ops.tensor_tensor(Y[:, b, 0, :, :], Y[:, b, 0, :, :], Y[:, b, 1, :, :], ALU.add).then_inc(s[added], 1)
            eng.wait_ge(s[added], n + 1)
            ops.tensor_tensor(Y[:, b, 0, :, :], Y[:, b, 0, :, :], GBr[:, b:b + 1, :].to_broadcast([P, C, D]), ALU.mult).then_inc(s[scaled], 1)
            eng.wait_ge(s[scaled], n + 1)
            ops.tensor_tensor(X[:, b, :, :], Y[:, b, 0, :, :], X[:, b, :, :], ALU.add).then_inc(s[done], 1)

        @block.sync
        def _(sp):
            xv = x.rearrange("b (c p) d -> p b c d", p=P)
            sp.dma_start(CT[:], cT).then_inc(s["c_in"], 16)
            sp.dma_start(X[:, 0, :, :], xv[:, 0, :, :]).then_inc(s["xin0"], 16)
            sp.dma_start(Wmod[:], wmod).then_inc(s["wmod_in"], 16)
            for dst, src in ((Wq, wq), (Wk, wk), (Wvg, wvg), (W1k, gk_w1), (W2k, gk_w2), (Gb, gk_b)):
                sp.dma_start(dst[:], src).then_inc(s["proj_in"], 16)
            sp.dma_start(X[:, 1, :, :], xv[:, 1, :, :]).then_inc(s["xin1"], 16)
            sp.dma_start(X[:, 2:, :, :], xv[:, 2:, :, :]).then_inc(s["xin2"], 16)
            sp.dma_start(WoR, wo).then_inc(s["attn_in"], 16)
            sp.dma_start(Rw[:], rwT).then_inc(s["attn_in"], 16)
            for j in range(2):
                sp.dma_start(RmsW[j * HV:(j + 1) * HV, :], rms_w).then_inc(s["attn_in"], 16)

            def stage_weights(e):
                sp.dma_start(Stage[:, 0, :], w1T[:, e, :]).then_inc(s["stage"], 16)
                sp.dma_start(Stage[:, 1, :], w2T[:, e, :]).then_inc(s["stage"], 16)

            stage_weights(0)
            with sp.Fori(0, E - 1) as e:
                wait(sp, "w_lo", e * 2 + 2)
                stage_weights(e + 1)
            sp.wait_ge(s["padrow"], 2)
            pad = PadRow[:]
            sp.dma_start(rows_dram[SPARE:SPARE + BT, :].rearrange("(j p) d -> p j d", p=P), pad).then_inc(s["pads"], 16)
            sp.wait_ge(s["pad_at"], 1)
            for e in range(E):
                at = sp.value_load(PadAt[0:1, e:e + 1], min_val=e * REG, max_val=e * REG + N)
                sp.dma_start(rows_dram[bass.ds(at, BT), :].rearrange("(j p) d -> p j d", p=P), pad).then_inc(s["pads"], 16)

            def first_row(j):
                return sp.value_load(Tab[0:1, 0, j:j + 1] if isinstance(j, int) else Tab[0:1, 0, bass.ds(j, 1)], min_val=0, max_val=SPARE)

            def load(at, r):
                sp.dma_start(XR[r][:], rows_dram[bass.ds(at, BT), :].rearrange("(j p) d -> p j d", p=P)).then_inc(s[f"xblk{r}"], 16)

            sp.wait_ge(s["tab_row"], 1)
            rows = [first_row(r) for r in range(RING)]
            sp.wait_ge(s["pads"], 16 * (E + 1))
            for u in range(2):
                sp.wait_ge(s[f"scat{u}"], 16 * TOP * C * B // 2)
            for r in range(RING):
                load(rows[r], r)

            def next_load(j, r):
                wait(sp, "xt_ps", j + (1 - RING))
                wait(sp, "ids", j + (1 - RING))
                load(first_row(j), r)

            with sp.Fori(0, NBLK // RING - 1) as i:
                for r in range(RING):
                    next_load(i * RING + (RING + r), r)
            for j in range(NBLK // RING * RING, NBLK):
                next_load(j, j % RING)
            for r in range(RING):
                sp.wait_ge(s[f"ysc{r}"], 16 * BH * len(range(r, NBLK, RING)))
            yv = y_dram.rearrange("(k b c p) d -> p b k c d", p=P, c=C, b=B)
            for b in range(B):
                for k in range(TOP):
                    sp.dma_start(Y[:, b, k, :, :], yv[:, b, k, :, :]).then_inc(s[f"y_in{b}"], 16)
            ov = out.rearrange("b (c p) d -> p b c d", p=P)
            for b in range(B):
                if b in POOL_OUT:
                    sp.wait_ge(s["yfin_p"], POOL_OUT.index(b) + 1)
                else:
                    sp.wait_ge(s["yfin"], DVE_OUT.index(b) + 1)
                sp.dma_start(ov[:, b, :, :], X[:, b, :, :]).then_inc(s["out_dma"], 16)
            sp.wait_ge(s["out_dma"], 16 * B)

        @block.gpsimd
        def _(pool):
            nc.gpsimd.memset(Id[:], 0.0).then_inc(s["ident_a"], 1)
            nc.gpsimd.memset(Causal[:], 1.0).then_inc(s["ident_a"], 1)
            nc.gpsimd.memset(Earlier[:], 1.0).then_inc(s["ident_a"], 1)
            nc.gpsimd.memset(Restart[:], 1.0).then_inc(s["ident_a"], 1)
            nc.gpsimd.memset(Before[:], 1.0).then_inc(s["ident_a"], 1)
            nc.gpsimd.memset(EpsC[:], EPS).then_inc(s["const"], 1)
            nc.gpsimd.memset(Ones[:], 1.0).then_inc(s["const"], 1)
            pool.wait_ge(s["ident_a"], 5)
            nc.gpsimd.affine_select(out=Id[:], in_=Id[:], compare_op=ALU.not_equal, fill=1.0, base=0,
                                    pattern=[[-1, P]], channel_multiplier=1).then_inc(s["ident"], 1)
            nc.gpsimd.affine_select(out=Causal[:], in_=Causal[:], compare_op=ALU.is_ge, fill=0.0, base=0,
                                    pattern=[[1, P]], channel_multiplier=-1).then_inc(s["const"], 1)
            nc.gpsimd.affine_select(out=Earlier[:], in_=Earlier[:], compare_op=ALU.is_gt, fill=0.0, base=0,
                                    pattern=[[1, P]], channel_multiplier=-1).then_inc(s["const"], 1)
            nc.gpsimd.memset(Restart[:, :, 0:1], 0.0).then_inc(s["const"], 1)
            nc.gpsimd.affine_select(out=Before[:], in_=Before[:], compare_op=ALU.is_gt, fill=0.0, base=0,
                                    pattern=[[1, E], [-1, E]], channel_multiplier=0).then_inc(s["const"], 1)
            nc.gpsimd.iota(Place[:], pattern=[[T, B], [N, TOP], [P, C]], base=0, channel_multiplier=1).then_inc(s["const"], 1)
            nc.gpsimd.iota(RegE[:], pattern=[[REG, E]], base=0, channel_multiplier=0,
                           allow_small_or_imprecise_dtypes=True).then_inc(s["const"], 1)
            nc.gpsimd.iota(Jn[:], pattern=[[1, NBLK]], base=0, channel_multiplier=0,
                           allow_small_or_imprecise_dtypes=True).then_inc(s["const"], 1)
            nc.gpsimd.memset(KT[:], 0.0).then_inc(s["const"], 1)
            nc.gpsimd.memset(Count[:], 0.0).then_inc(s["const"], 1)
            nc.gpsimd.memset(PadRow[:], 0.0).then_inc(s["padrow"], 1)
            pool.wait_ge(s["padrow"], 1)
            nc.gpsimd.iota(PadRow[:, :, D:D + 1].bitcast(I32), pattern=[[P, BH], [0, 1]], base=TOP * N,
                           channel_multiplier=1).then_inc(s["padrow"], 1)

            pool.wait_ge(s["attn_in"], 64)
            nc.gpsimd.tensor_tensor(Wo[:], WoR, RmsW[:].rearrange("p (o i) -> p o i", o=1).to_broadcast([P, 2, D]),
                                    ALU.mult).then_inc(s["wo_fin"], 1)

            def carry_wait():
                nc.gpsimd.tensor_tensor(PadP[:], Id[:, 0:1], Id[:, 0:1], ALU.mult).then_inc(s["held"], 1)

            def keys(b, u):
                wait(pool, "wo_fin", 1)
                wait(pool, "expq", 2 * b + 2)
                wait(pool, "q_sb", b + 1)
                wait(pool, "qblk", H * b)
                nc.gpsimd.tensor_tensor(QE[:], Q[:], ExpQ[:, 0, :], ALU.mult).then_inc(s["qe"], 1)

            def queries_start(b, u):
                wait(pool, "expb", b + 1)
                wait(pool, "o_ps", C * b)
                nc.gpsimd.tensor_tensor(QS[:], Q[:], ExpB[:], ALU.mult).then_inc(s["qs"], 1)

            def outgate(b, u):
                wait(pool, "sigg", b + 1)
                nc.gpsimd.tensor_tensor(AbsG[:], Gate, AbsG[:], ALU.mult).then_inc(s["gate"], 1)

            def low_parts(b, u):
                wait(pool, "w_hi", 2 * b + 2)
                nc.gpsimd.tensor_tensor(W1[:, b, 1, :], Stage[:, 0, :], W1[:, b, 0, :].bitcast(F32), ALU.subtract).then_inc(s["w_lo"], 1)
                nc.gpsimd.tensor_tensor(W2[:, b, :, 1, :], Stage[:, 1, :].rearrange("p (k d) -> p k d", k=KH),
                                        W2[:, b, :, 0, :].bitcast(F32), ALU.subtract).then_inc(s["w_lo"], 1)

            def gate_output(b, u):
                if not last(b):
                    output_gate(pool, nc.gpsimd, b)

            def project(b, u):
                if not last(b):
                    add_attention(pool, nc.gpsimd, b)

            def rows(b, u):
                if not last(b):
                    modulate(pool, nc.gpsimd, b, u)

            def scatter(b, u):
                wait(pool, "held", b)
                wait(pool, "slotu", b + 1)
                wait(pool, "row_h", TOP * b + TOP)
                wait(pool, "row_id", b + 1)
                wait(pool, "w01", b + 1)
                carry_wait()
                for k in range(TOP):
                    for c in range(C):
                        nc.gpsimd.indirect_dma_start(
                            rows_dram, bass.IndirectOffsetOnAxis(ap=SlotI[u][:, k, c:c + 1], axis=0), HR[u][:, k, c, :], None,
                            bounds_check=ROWS - 1, oob_is_err=False).then_inc(s[f"scat{u}"], 16)

            pipeline(pool, (
                "p1_keys+1 p1_starts+1 p2_project+0 p3_scatter-1 p1_outgate+1 p3_rows+0 p2_weights+1 "
                "p2_outgate+1"),
                     p1_keys=keys, p1_starts=queries_start, p1_outgate=outgate, p2_weights=low_parts, p2_outgate=gate_output,
                     p2_project=project, p3_rows=rows, p3_scatter=scatter)

            def c(j, r, turn):
                wait(pool, "held", j + B)
                wait(pool, f"ys{r % 2}", turn * (BH * RING // 2) + (r // 2 + 1) * BH)
                carry_wait()
                for half in range(BH):
                    nc.gpsimd.indirect_dma_start(
                        y_dram, bass.IndirectOffsetOnAxis(ap=Ids[r][:, half, 0:1], axis=0), YS[r][:, half, :], None,
                        bounds_check=TOP * N - 1, oob_is_err=False).then_inc(s[f"ysc{r}"], 16)

            run_blocks(pool, block_pipeline(nothing, nothing, c))
            pool.wait_ge(s["gb_row"], B)
            for n, b in enumerate(POOL_OUT):
                result(pool, nc.gpsimd, b, n, ("ysum_p", "ygb_p", "yfin_p"))

        @block.scalar
        def _(act):
            nc.scalar.preload_act_table_set("natural_log_exp_and_others")
            act.wait_ge(s["c_in"], 16)
            nc.scalar.activation(SC[:, 0, :], CT[:], ACT.Abs).then_inc(s["silu_act"], 1)
            act.wait_ge(s["silu_act"], 1)
            nc.scalar.activation(SC[:, 1, :], SC[:, 0, :], ACT.Exp, scale=-1.0).then_inc(s["silu_act"], 1)
            act.wait_ge(s["silu_act"], 2)
            nc.scalar.activation(SC[:, 2, :], SC[:, 1, :], ACT.Ln, bias=1.0).then_inc(s["silu_act"], 1)
            act.wait_ge(s["silu_dve"], 1)
            nc.scalar.activation(SC[:, 3, :], SC[:, 3, :], ACT.Exp).then_inc(s["silu_act"], 1)
            act.wait_ge(s["cols_ps"], 1)
            nc.scalar.activation(Cols[:, 0, :], psT[:, 0:B], ACT.Copy).then_inc(s["cols"], 1)
            nc.scalar.activation(Cols[:, 1, :], psT[:, B:2 * B], ACT.Identity, bias=1.0).then_inc(s["cols"], 1)

            def rstd(b, k, mv, lnv, out):
                wait(act, mv, C * b + C)
                nc.scalar.activation(LnV[:, k, :], MV[:, k, :, 1], ACT.Ln, bias=EpsC[:]).then_inc(s[lnv], 1)
                wait(act, lnv, b + 1)
                nc.scalar.activation(Rstd[:, k, :], LnV[:, k, :], ACT.Exp, scale=-0.5).then_inc(s[out], 1)

            def norm1(b, u):
                rstd(b, 0, "mv1", "lnv1", "rstd1")

            def norm2(b, u):
                rstd(b, 1, "mv2", "lnv2", "rstd2")

            def transpose(b, u):
                wait(act, "cols", 2)
                wait(act, "xT1", b + 1)
                nc.scalar.activation(HT[:], psT[:], ACT.Identity, scale=Cols[:, 1, bass.ds(b, 1)],
                                     bias=Cols[:, 0, bass.ds(b, 1)]).then_inc(s["hT"], 1)

            def query(b, u):
                wait(act, "uT_ps", b + 1)
                nc.scalar.copy(UT[:], pjA[0:LR, :]).then_inc(s["uT"], 1)

            def query_copy(b, u):
                wait(act, "q_ps", b + 1)
                wait(act, "qs", b)
                nc.scalar.mul(Q[:], pjB[:], float(HK ** -0.5)).then_inc(s["q_sb"], 1)

            def gates(b, u):
                wait(act, "gl_ps", b + 1)
                wait(act, "cum", b)
                nc.scalar.activation(GL[:], pjA[:], ACT.Identity, bias=Gb[:]).then_inc(s["gl_sb"], 1)

            def keys_copy(b, u):
                wait(act, "k_ps", b + 1)
                wait(act, "ktil", (NS + 1) * b)
                nc.scalar.copy(K[:], pjB[:].rearrange("p (c t) -> p c t", c=C)).then_inc(s["k_sb"], 1)

            def log_gates(b, u):
                wait(act, "gl_sb", b + 1)
                nc.scalar.activation(Ln1[:], GL[:], ACT.Abs).then_inc(s["abs1"], 1)
                wait(act, "abs1", b + 1)
                nc.scalar.activation(Ln1[:], Ln1[:], ACT.Exp, scale=-1.0).then_inc(s["ex1"], 1)
                wait(act, "ex1", b + 1)
                nc.scalar.activation(Ln1[:], Ln1[:], ACT.Ln, bias=1.0).then_inc(s["ln1"], 1)

            def values(b, u, chunks):
                wait(act, "o_ps", C * b)
                wait(act, "gate", b)
                for c in chunks:
                    wait(act, "vg_ps", C * b + c + 1)
                    nc.scalar.copy(VG[:, c, :], (pjA, pjB)[c % 2][:]).then_inc(s["vg"], 1)

            def differences(b, u):
                for i in range(NS):
                    wait(act, "difk", NS * b + i + 1)
                    k = KT[:, :, i, 0:SUB * (i + 1)]
                    nc.scalar.activation(k, k, ACT.Exp, scale=1.0 / GATE_NORM).then_inc(s["expk"], 1)

            def decays(b, u):
                for k in range(2):
                    wait(act, "difq", 2 * b + k + 1)
                    nc.scalar.activation(ExpQ[:, k, :], ExpQ[:, k, :], ACT.Exp, scale=1.0 / GATE_NORM).then_inc(s["expq"], 1)

            def decays_start(b, u):
                wait(act, "qs", b)
                wait(act, "s_st", 3 * b)
                nc.scalar.activation(Decay[:], Cum[:, :, NS - 1, SUB - 1], ACT.Exp, scale=1.0 / GATE_NORM).then_inc(s["decay"], 1)
                nc.scalar.activation(ExpB[:], Cum[:], ACT.Exp, scale=1.0 / GATE_NORM).then_inc(s["expb"], 1)

            def keys(b, u):
                wait(act, "qe", b + 1)
                wait(act, "sc_ps", C * b)
                for h in range(H):
                    nc.scalar.activation(QB[:, h, :], QE[:], ACT.Copy, scale=HeadMask[:, h, 0:1]).then_inc(s["qblk"], 1)

            def outgate(b, u):
                wait(act, "vg", C * b + C)
                wait(act, "ogat", b)
                nc.scalar.activation(AbsG[:], Gate, ACT.Abs).then_inc(s["absg"], 1)
                wait(act, "absg", b + 1)
                nc.scalar.activation(AbsG[:], AbsG[:], ACT.Exp, scale=-1.0).then_inc(s["exg"], 1)
                wait(act, "exg", b + 1)
                nc.scalar.activation(AbsG[:], AbsG[:], ACT.Ln, bias=1.0).then_inc(s["lng"], 1)

            def outgate_exp(b, u):
                wait(act, "ming", b + 1)
                nc.scalar.activation(AbsG[:], AbsG[:], ACT.Exp).then_inc(s["sigg"], 1)

            def scores(b, u):
                wait(act, "ket_ps", b + 1)
                nc.scalar.copy(KEt[:], psK[:, 0:3 * P].rearrange("p (c k) -> p c k", c=3)).then_inc(s["ket"], 1)

            def modulation(b, u):
                wait(act, "rows_ps", b + 1)
                wait(act, "h2", 2 * b - 2)
                nc.scalar.copy(Rows[u][:], psT[:].rearrange("p (j d) -> p j d", j=4)).then_inc(s["rows"], 1)

            def state(b, u):
                wait(act, "stage", b * 32 + 32)
                nc.scalar.copy(W1[:, b, 0, :], Stage[:, 0, :]).then_inc(s["w_hi"], 1)
                nc.scalar.copy(W2[:, b, :, 0, :], Stage[:, 1, :].rearrange("p (k d) -> p k d", k=KH)).then_inc(s["w_hi"], 1)

            def output(b, u, half):
                wait(act, "o_ps", C * b + 2 * half + 2)
                wait(act, "oT_ps", 2 * b)
                nc.scalar.copy(O[:, 2 * half:2 * half + 2, :],
                               psO[:].rearrange("p (c v) -> p c v", c=2)).then_inc(s["o_sb"], 1)

            def squares(b, u):
                wait(act, "o_sb", 2 * b + 2)
                wait(act, "at_ps", b)
                nc.scalar.activation(Sq, O[:], ACT.Square).then_inc(s["sq"], 1)

            def gb_rows(b, u):
                wait(act, "rows_fin", b + 1)
                nc.scalar.copy(GBr[:, b, :], Rows[u][:, 3, :]).then_inc(s["gb_row"], 1)

            def rms(b, u):
                wait(act, "ms", b + 1)
                nc.scalar.activation(Ms[:, 1, :], Ms[:, 0, :], ACT.Ln, scale=1.0 / HV, bias=EpsC[:]).then_inc(s["lnms"], 1)
                wait(act, "lnms", b + 1)
                nc.scalar.activation(Ms[:, 1, :], Ms[:, 1, :], ACT.Exp, scale=-0.5).then_inc(s["rms"], 1)

            def output_transpose(b, u, j):
                wait(act, "oT_ps", 2 * b + j + 1)
                nc.scalar.copy(OT[:, j, :], (psS0, psS1)[j][:]).then_inc(s["oT"], 1)

            def logits(b, u):
                wait(act, "xT2", b + 1)
                nc.scalar.copy(H2T[:], psT[:]).then_inc(s["h2T"], 1)

            def rank(b, u):
                wait(act, "sh", b + 1)
                nc.scalar.activation(Sm[:, 1, :, :], Sm[:, 0, :, :], ACT.Exp).then_inc(s["ex"], 1)

            pipeline(act, (
                "p1_outgate+0 p2_keysT+0 p1_outexp+0 p1_norm+1 p2_rows+0 p2_weights+0 p1_transpose+1 "
                "p2_output01+0 p1_rank+1 p1_query+1 p3_norm-1 p1_gates+1 p1_keycopy+1 p1_loggates+1 "
                "p2_output23+0 p2_squares+0 p1_values01+1 p3_logits-1 p2_gbrow+0 p2_rms+0 p1_values23+1 "
                "p1_differences+1 p1_decays+1 p2_transpose0+0 p2_transpose1+0 p1_starts+1 p3_rank-1 "
                "p1_keys+1"),
                     p1_norm=norm1, p1_transpose=transpose, p1_rank=query, p1_query=query_copy, p1_gates=gates,
                     p1_keycopy=keys_copy, p1_loggates=log_gates, p1_values01=part(values, range(0, 2)),
                     p1_values23=part(values, range(2, 4)), p1_differences=differences, p1_decays=decays,
                     p1_starts=decays_start, p1_keys=keys, p1_outgate=outgate, p1_outexp=outgate_exp,
                     p2_keysT=scores, p2_rows=modulation, p2_weights=state, p2_output01=part(output, 0),
                     p2_output23=part(output, 1), p2_squares=squares, p2_gbrow=gb_rows, p2_rms=rms,
                     p2_transpose0=part(output_transpose, 0), p2_transpose1=part(output_transpose, 1),
                     p3_norm=norm2, p3_logits=logits, p3_rank=rank)

            def b(j, r, turn):
                for n in range(HB):
                    k = slice(n * KB, (n + 1) * KB)
                    wait(act, "h_ps", j * HB + (n + 1))
                    if n == 0:
                        wait(act, "g_lo", j * HB - HB)
                    nc.scalar.activation(G[r % 2][:, k, :], psH[r % 2][n][:].rearrange("p (k t) -> p k t", k=KB),
                                         ACT.Gelu).then_inc(s["gelu"], 1)
                    if n == 0:
                        wait(act, "y_ps", j - 1)
                    wait(act, "gelu", j * HB + (n + 1))
                    nc.scalar.copy(Ghi[r % 2][:, k, :], G[r % 2][:, k, :]).then_inc(s["g_hi"], 1)

            def a(j, r, turn):
                wait(act, "xt_ps", j + 1)
                wait(act, "h_ps", j * HB - HB)
                nc.scalar.copy(XThi[r % 2][:], psX[r % 2][:, 0:BT]).then_inc(s["xt_hi"], 1)

            def c(j, r, turn):
                wait(act, "y_ps", j + 1)
                wait(act, f"ysc{r}", turn * (16 * BH))
                y = psY[r % 2][:].rearrange("p (h a d) -> p h a d", h=BH, a=2)
                wait(act, "ids", j + 1)
                for half in range(BH):
                    nc.scalar.activation(YS[r][:, half, :], y[:, half, 0, :], ACT.Copy,
                                         scale=Ids[r][:, half, 1:2].bitcast(F32)).then_inc(s["yhi"], 1)

            run_blocks(act, block_pipeline(a, b, c))

        @block.vector
        def _(dve):
            v = nc.vector
            dve.wait_ge(s["silu_act"], 3)
            v.scalar_tensor_tensor(SC[:, 3, :], CT[:], 0.0, SC[:, 2, :], ALU.min, ALU.subtract).then_inc(s["silu_dve"], 1)
            dve.wait_ge(s["silu_act"], 4)
            v.tensor_tensor(SilC[:], CT[:], SC[:, 3, :], ALU.mult).then_inc(s["silu_dve"], 1)
            dve.wait_ge(s["silu_dve"], 2)
            v.memset(HeadMask[:], 0.0).then_inc(s["hmask"], 1)
            dve.wait_ge(s["hmask"], 1)
            for h in range(H):
                v.memset(HeadMask[h * HK:(h + 1) * HK, h, :], 1.0).then_inc(s["hmask"], 1)
            dve.wait_ge(s["hmask"], 1 + H)
            dve.wait_ge(s["const"], 11)

            def stats(b, k, src, names):
                bn, mv, rs, done = names
                for c in range(C):
                    v.bn_stats(St6[:, k, c, :], src[:, c, :]).then_inc(s[bn], 1)
                wait(dve, bn, C * b + C)
                v.memset(Pad[:], 0.0)
                for c in range(C):
                    v.bn_aggr(MV[:, k, c, :], St6[:, k, c, :]).then_inc(s[mv], 1)

            def norm(b, k, src, out, names):
                bn, mv, rs, done = names
                wait(dve, rs, b + 1)
                for c in range(C):
                    v.tensor_scalar(out[:, c, :], src[:, c, :], MV[:, k, c, 0:1], Rstd[:, k, c:c + 1],
                                    ALU.subtract, ALU.mult).then_inc(s[done], 1)

            names1, names2 = ("bn1", "mv1", "rstd1", "xhat1"), ("bn2", "mv2", "rstd2", "xhat2")

            def stats1(b, u):
                dve.wait_ge(s[f"xin{b}" if isinstance(b, int) and b < 2 else "xin2"], 16)
                stats(b, 0, X[:, b, :, :], names1)

            def norm1(b, u):
                wait(dve, "xT1", b)
                norm(b, 0, X[:, b, :, :], Xh, names1)

            def stats2(b, u):
                wait(dve, "x2", b + 1)
                v.memset(Pad[:], 0.0)
                stats(b, 1, X[:, b, :, :], names2)

            def norm2(b, u):
                wait(dve, "xT2", b)
                wait(dve, "row_h", TOP * b)
                norm(b, 1, X[:, b, :, :], H2, names2)
                if last(b):
                    modulate(dve, v, b, u)

            def values(b, u):
                wait(dve, "ln1", b + 1)
                v.scalar_tensor_tensor(GL[:], GL[:], 0.0, Ln1[:], ALU.min, ALU.subtract).then_inc(s["g16"], 1)

            def sums(b, u):
                wait(dve, "g16", b + 1)
                wait(dve, "expb", b)
                v.tensor_tensor_scan(Cum[:].rearrange("p c i s -> p (c i s)"), Restart[:].rearrange("p c t -> p (c t)"),
                                     GL[:], 0.0, ALU.mult, ALU.add).then_inc(s["cum"], 1)

            def differences(b, u):
                wait(dve, "cum", b + 1)
                wait(dve, "sc_ps", C * b)
                for i in range(NS):
                    ref = Cum[:, :, i, SUB // 2 - 1:SUB // 2].to_broadcast([P, C, SUB * (i + 1)])
                    v.tensor_tensor(KT[:, :, i, 0:SUB * (i + 1)], ref,
                                    Cum[:, :, 0:i + 1, :].rearrange("p c i s -> p c (i s)"), ALU.subtract).then_inc(s["difk"], 1)

            def differences_q(b, u):
                wait(dve, "qe", b)
                wait(dve, "ktil", (NS + 1) * b)
                v.tensor_tensor(ExpQ[:, 0, :].rearrange("p (c i s) -> p (c i) s", c=C, i=NS), Cum[:].rearrange("p c i s -> p (c i) s"),
                                Cum[:, :, :, SUB // 2 - 1:SUB // 2].rearrange("p c i s -> p (c i) s").to_broadcast([P, C * NS, SUB]),
                                ALU.subtract).then_inc(s["difq"], 1)
                v.tensor_tensor(ExpQ[:, 1, :].rearrange("p (c t) -> p c t", c=C),
                                Cum[:, :, NS - 1, SUB - 1:SUB].to_broadcast([P, C, P]),
                                Cum[:].rearrange("p c i s -> p c (i s)"), ALU.subtract).then_inc(s["difq"], 1)

            def keys(b, u, refs):
                wait(dve, "k_sb", b + 1)
                for i in refs:
                    wait(dve, "expk", NS * b + i + 1)
                    k = KT[:, :, i, 0:SUB * (i + 1)]
                    v.tensor_tensor(k, k, K[:, :, 0:SUB * (i + 1)], ALU.mult).then_inc(s["ktil"], 1)

            def keys_end(b, u):
                wait(dve, "expq", 2 * b + 2)
                wait(dve, "ket_ps", b)
                v.tensor_tensor(KE[:], K[:], ExpQ[:, 1, :].rearrange("p (c t) -> p c t", c=C), ALU.mult).then_inc(s["ktil"], 1)

            def outgate(b, u):
                wait(dve, "lng", b + 1)
                v.scalar_tensor_tensor(AbsG[:], Gate, 0.0, AbsG[:], ALU.min, ALU.subtract).then_inc(s["ming"], 1)

            hm = HeadMask[:].rearrange("p h v -> p (h v)")
            cm = Causal[:].rearrange("p (o t) -> p o t", o=1).to_broadcast([P, H, P])

            def masked(b, u, c):
                wait(dve, "sc_ps", C * b + c + 1)
                if c >= 2:
                    wait(dve, "o_ps", C * b + c - 1)
                v.tensor_tensor(PT[c % 2][:], (psS0, psS1)[c % 2][:].rearrange("p (h t) -> p h t", h=H), cm,
                                ALU.mult).then_inc(s["pt"], 1)

            def scores(b, u):
                wait(dve, "rows_ps", b)
                v.tensor_copy(SilB[:], SilC[:, bass.ds(b, 1)].to_broadcast([P, P])).then_inc(s["silu_b"], 1)

            def state(b, u):
                wait(dve, "ds_ps", b + 1)
                v.tensor_tensor(S[0][:], psD[:, 0:DV], hm, ALU.mult).then_inc(s["s_st"], 1)
                wait(dve, "rows_used", b)
                for c in (1, 2):
                    v.tensor_tensor(Stmp[:, c - 1, :], psD[:, DV:2 * DV] if c == 1 else psK[:, 0:DV], hm,
                                    ALU.mult).then_inc(s["s_tmp"], 1)
                for c in (1, 2):
                    wait(dve, "s_tmp", 2 * b + c)
                    wait(dve, "s_st", 3 * b + c)
                    v.scalar_tensor_tensor(S[c][:], S[c - 1][:], Decay[:, c:c + 1], Stmp[:, c - 1, :],
                                           ALU.mult, ALU.add).then_inc(s["s_st"], 1)

            def output(b, u):
                wait(dve, "rows", b + 1)
                wait(dve, "s_st", 3 * b + 3)
                gates, sg, ab = Rows[u][:, 0:4:3, :], Sgn[:, 0:2, :], Sgn[:, 2:4, :]
                v.tensor_scalar(sg, gates, 0.0, 2.0, ALU.is_ge, ALU.mult).then_inc(s["rows_ab"], 1)
                v.tensor_scalar(ab, gates, -1.0, None, ALU.mult).then_inc(s["rows_ab"], 1)
                wait(dve, "rows_ab", 2 * b + 2)
                v.scalar_tensor_tensor(ab, gates, 0.25, ab, ALU.max, ALU.max).then_inc(s["rows_mul"], 1)

            def row_gates(b, u):
                wait(dve, "rows_mul", b + 1)
                gates, sg, ab = Rows[u][:, 0:4:3, :], Sgn[:, 0:2, :], Sgn[:, 2:4, :]
                v.scalar_tensor_tensor(gates, sg, -1.0, ab, ALU.add, ALU.mult).then_inc(s["rows_used"], 1)
                v.tensor_scalar(Rows[u][:, 2, :], Rows[u][:, 2, :], 1.0, None, ALU.add).then_inc(s["rows_fin"], 1)

            def rms(b, u):
                wait(dve, "sq", b + 1)
                v.tensor_reduce(Ms[:, 0, :], Sq.rearrange("p c (h v) -> p (c h) v", h=H), axis=AX.X, op=ALU.add).then_inc(s["ms"], 1)

            def rms_norm(b, u):
                if last(b):
                    output_gate(dve, v, b)
                wait(dve, "ogat", b + 1)
                wait(dve, "rms", b + 1)
                v.tensor_tensor(O[:].rearrange("p c (h v) -> p (c h) v", h=H), O[:].rearrange("p c (h v) -> p (c h) v", h=H),
                                Ms[:, 1, :].rearrange("p (n o) -> p n o", o=1).to_broadcast([P, C * H, HV]), ALU.mult).then_inc(s["onrm"], 1)

            def project(b, u):
                wait(dve, "at_ps", b + 1)
                wait(dve, "x2", b)
                wait(dve, "rows_used", b + 1)
                v.tensor_tensor(At[:], psO[:].rearrange("p (c d) -> p c d", c=C), Rows[u][:, 0:1, :].to_broadcast([P, C, D]),
                                ALU.mult).then_inc(s["at_g"], 1)
                if last(b):
                    add_attention(dve, v, b)

            def rows(b, u):
                wait(dve, f"scat{u}", (b - u) * (16 * TOP * C // 2))
                v.tensor_copy(HR[u][:, :, :, D:D + 1].rearrange("p k c o -> p k (c o)").bitcast(I32), Place[:, b, :, :]).then_inc(s["row_id"], 1)

            def logits(b, u):
                wait(dve, "h2", 2 * b + 2)
                for k in range(TOP):
                    v.tensor_copy(HR[u][:, k, :, 0:D], H2[:]).then_inc(s["row_h"], 1)

            def logits_copy(b, u):
                wait(dve, "lg_ps", b + 1)
                v.tensor_copy(LG[:], psT[:, 0:C * E].rearrange("p (c e) -> p c e", c=C)).then_inc(s["lg"], 1)

            def rank(b, u):
                wait(dve, "lg", b + 1)
                mine = LG[:].rearrange("p c (e o) -> p c e o", o=1).to_broadcast([P, C, E, E])
                other = LG[:].rearrange("p c (o e) -> p c o e", o=1).to_broadcast([P, C, E, E])
                v.tensor_tensor(Rk[:, 0, :, :, :], other, mine, ALU.is_gt).then_inc(s["rk01"], 1)
                v.tensor_tensor(Rk[:, 1, :, :, :], other, mine, ALU.is_equal).then_inc(s["rk01"], 1)
                v.tensor_reduce(R1[:, 0, :], LG[:], axis=AX.X, op=ALU.max).then_inc(s["route"], 1)
                wait(dve, "rk01", 2 * b + 2)
                bf = Before[:].rearrange("p e j -> p (e j)").rearrange("p (o n) -> p o n", o=1).to_broadcast([P, C, E * E])
                rk = [Rk[:, j, :, :, :].rearrange("p c e j -> p c (e j)") for j in range(2)]
                v.tensor_tensor(rk[1], rk[1], bf, ALU.mult).then_inc(s["route"], 1)
                wait(dve, "route", 9 * b + 1)
                v.tensor_tensor(Sm[:, 0, :, :], LG[:], R1[:, 0, :].rearrange("p (c o) -> p c o", o=1).to_broadcast([P, C, E]),
                                ALU.subtract).then_inc(s["sh"], 1)
                wait(dve, "route", 9 * b + 2)
                v.tensor_tensor(rk[0], rk[0], rk[1], ALU.add).then_inc(s["route"], 1)
                wait(dve, "route", 9 * b + 3)
                v.tensor_reduce(Sm[:, 2, :, :].rearrange("p c e -> p (c e)"), Rk[:, 0, :, :, :].rearrange("p c e j -> p (c e) j"),
                                axis=AX.X, op=ALU.add).then_inc(s["rk4"], 1)
                wait(dve, "rk4", b + 1)
                rank = Sm[:, 2, :, :]
                v.tensor_scalar(Sel[:], rank, TOP - 0.5, None, ALU.is_lt).then_inc(s["sel"], 1)
                for k in range(TOP):
                    v.tensor_scalar(Sel2[:, k, :, :], rank, float(k), None, ALU.is_equal).then_inc(s["sel2"], 1)

            def counts(b, u):
                wait(dve, "count", b * C)
                wait(dve, "pos_ps", b)
                v.tensor_copy(Count[:, 0, :], Count[:, C, :]).then_inc(s["carry"], 1)
                wait(dve, "carry", b + 1)
                wait(dve, "sel", b + 1)
                for c in range(C):
                    wait(dve, "count", b * C + c)
                    v.tensor_tensor(Count[:, c + 1, :], Count[:, c, :], Sel[:, c, :], ALU.add).then_inc(s["count"], 1)

            def softmax(b, u):
                wait(dve, "ex", b + 1)
                v.tensor_reduce(R1[:, 1, :], Sm[:, 1, :, :], axis=AX.X, op=ALU.add).then_inc(s["route"], 1)
                wait(dve, "route", 9 * b + 4)
                v.reciprocal(R1[:, 2, :], R1[:, 1, :]).then_inc(s["route"], 1)
                wait(dve, "route", 9 * b + 5)
                v.tensor_tensor(Sm[:, 3, :, :], Sm[:, 1, :, :], R1[:, 2, :].rearrange("p (c o) -> p c o", o=1).to_broadcast([P, C, E]),
                                ALU.mult).then_inc(s["route"], 1)
                wait(dve, "route", 9 * b + 6)
                wait(dve, "sel2", b * TOP + TOP)
                flat = lambda a: a.rearrange("p c e -> p (c e)").rearrange("p (o n) -> p o n", o=1).to_broadcast([P, TOP, C * E])
                sel2 = Sel2[:].rearrange("p k c e -> p k (c e)")
                pick = [Pick[:, j, :, :, :].rearrange("p k c e -> p k (c e)") for j in range(2)]
                pickr = [Pick[:, j, :, :, :].rearrange("p k c e -> p (k c) e") for j in range(2)]
                v.tensor_tensor(pick[0], sel2, flat(Sm[:, 3, :, :]), ALU.mult).then_inc(s["route"], 1)
                wait(dve, "route", 9 * b + 7)
                wait(dve, f"scat{u}", (b - u) * (16 * TOP * C // 2))
                v.tensor_reduce(HR[u][:, :, :, D + 1:D + 2].rearrange("p k c o -> p (k c) o"),
                                Pick[:, 0, :, :, :].rearrange("p k c e -> p (k c) e"), axis=AX.X, op=ALU.add).then_inc(s["w01"], 1)

            def slots(b, u):
                flat = lambda a: a.rearrange("p c e -> p (c e)").rearrange("p (o n) -> p o n", o=1).to_broadcast([P, TOP, C * E])
                sel2 = Sel2[:].rearrange("p k c e -> p k (c e)")
                pick = [Pick[:, j, :, :, :].rearrange("p k c e -> p k (c e)") for j in range(2)]
                pickr = [Pick[:, j, :, :, :].rearrange("p k c e -> p (k c) e") for j in range(2)]
                wait(dve, "pos_ps", b + 1)
                v.tensor_tensor(Sm[:, 0, :, :], psT[:, 2 * C * E:3 * C * E].rearrange("p (c e) -> p c e", c=C),
                                RegE[:].rearrange("p (o e) -> p o e", o=1).to_broadcast([P, C, E]), ALU.add).then_inc(s["slot"], 1)
                wait(dve, "slot", b + 1)
                v.tensor_tensor(pick[1], sel2, flat(Sm[:, 0, :, :]), ALU.mult).then_inc(s["route"], 1)
                wait(dve, "route", 9 * b + 8)
                v.tensor_reduce(Slot[:].rearrange("p k c -> p (k c)"), pickr[1], axis=AX.X, op=ALU.add).then_inc(s["route"], 1)
                wait(dve, "route", 9 * b + 9)
                v.tensor_copy(SlotI[u][:], Slot[:]).then_inc(s["slotu"], 1)

            pipeline(dve, (
                "p1_stats+1 p2_mask0+0 p1_norm+1 p2_mask1+0 p2_state+0 p3_stats-1 p2_rows+0 p2_rowgates+0 "
                "p3_norm-1 p2_mask2+0 p3_places-1 p2_mask3+0 p1_loggates+1 p1_sums+1 p3_rows-1 "
                "p1_differences+1 p2_squares+0 p1_diffq+1 p2_rms+0 p3_logits-1 p1_keys01+1 p1_keys23+1 "
                "p3_rank-1 p1_keysend+1 p3_counts-1 p2_project+0 p3_softmax-1 p3_slots-1 p2_silu+1 "
                "p1_outgate+1"),
                     p1_stats=stats1, p1_norm=norm1, p1_loggates=values, p1_sums=sums, p1_differences=differences,
                     p1_diffq=differences_q, p1_keys01=part(keys, range(0, 2)), p1_keys23=part(keys, range(2, 4)),
                     p1_keysend=keys_end, p1_outgate=outgate, p2_silu=scores, p2_mask0=part(masked, 0),
                     p2_mask1=part(masked, 1), p2_state=state, p2_rows=output, p2_rowgates=row_gates,
                     p2_mask2=part(masked, 2), p2_mask3=part(masked, 3),
                     p2_squares=rms, p2_rms=rms_norm, p2_project=project, p3_stats=stats2, p3_norm=norm2,
                     p3_places=rows, p3_rows=logits, p3_logits=logits_copy, p3_rank=rank, p3_counts=counts,
                     p3_softmax=softmax, p3_slots=slots)

            chain = [0]

            def link(ins):
                chain[0] += 1
                ins.then_inc(s["table"], 1)
                dve.wait_ge(s["table"], chain[0])

            dve.wait_ge(s["cnt_ps"], 1)
            dve.wait_ge(s["w_lo"], TOP * E)
            link(v.tensor_copy(Nb[:, 0, :], psT[:, 0:E]))
            v.tensor_tensor(PadAt[:], Nb[:, 0, :], RegE[:], ALU.add).then_inc(s["pad_at"], 1)
            link(v.tensor_scalar(NbI[:, 0, :], Nb[:, 0, :], float(BT - 1), None, ALU.add))
            link(v.tensor_scalar(NbI[:, 1, :], NbI[:, 0, :], BT.bit_length() - 1, None, ALU.logical_shift_right))
            link(v.tensor_copy(Nb[:, 1, :], NbI[:, 1, :]))
            link(v.tensor_tensor_scan(Nb[:, 2, :], Ones[:, 0:E], Nb[:, 1, :], 0.0, ALU.mult, ALU.add))
            ends = Nb[:, 2, :].rearrange("p (o e) -> p o e", o=1).to_broadcast([P, NBLK, E])
            jn = Jn[:].rearrange("p (j o) -> p j o", o=1).to_broadcast([P, NBLK, E])
            link(v.tensor_tensor(Le[:, 0, :, :], ends, jn, ALU.is_le))
            link(v.tensor_reduce(Bl[:, 0, :], Le[:, 0, :, :], axis=AX.X, op=ALU.add))
            v.tensor_scalar(Tab[:, 1, :], Bl[:, 0, :], float(E - 1), None, ALU.min).then_inc(s["tab_e"], 1)
            link(v.tensor_tensor(Le[:, 1, :, :], Le[:, 0, :, :], Nb[:, 1, :].rearrange("p (o e) -> p o e", o=1).to_broadcast([P, NBLK, E]), ALU.mult))
            link(v.tensor_reduce(Bl[:, 1, :], Le[:, 1, :, :], axis=AX.X, op=ALU.add))
            link(v.tensor_tensor(Bl[:, 2, :], Jn[:], Bl[:, 1, :], ALU.subtract))
            link(v.tensor_scalar(Bl[:, 3, :], Bl[:, 0, :], float(REG), None, ALU.mult))
            link(v.scalar_tensor_tensor(Bl[:, 0, :], Bl[:, 2, :], float(BT), Bl[:, 3, :], ALU.mult, ALU.add))
            v.tensor_scalar(Tab[:, 0, :], Bl[:, 0, :], float(SPARE), None, ALU.min).then_inc(s["tab_row"], 1)

            def a(j, r, turn):
                wait(dve, "h_ps", j * HB - HB)
                at = dve.value_load(Tab[0:1, 1, j:j + 1] if isinstance(j, int) else Tab[0:1, 1, bass.ds(j, 1)],
                                    min_val=0, max_val=E - 1)
                v.tensor_copy(W1b[r % 2][:], W1[:, bass.ds(at, 1), :, :].rearrange("p o a n -> p (o a) n")).then_inc(s["w1_b"], 1)
                wait(dve, "xt_ps", j + 1)
                wait(dve, f"ysc{r}", turn * (16 * BH))
                v.tensor_copy(Ids[r][:], XR[r][:, :, D:RW].bitcast(U32)).then_inc(s["ids"], 1)
                wait(dve, "xt_hi", j + 1)
                v.tensor_tensor(XTlo[r % 2][:], psX[r % 2][:, 0:BT], XThi[r % 2][:].bitcast(F32), ALU.subtract).then_inc(s["xt_lo"], 1)

            def b(j, r, turn):
                for n in range(HB):
                    wait(dve, "g_hi", j * HB + (n + 1))
                    k = slice(n * KB, (n + 1) * KB)
                    v.tensor_tensor(Glo[r % 2][:, k, :], G[r % 2][:, k, :], Ghi[r % 2][:, k, :].bitcast(F32),
                                    ALU.subtract).then_inc(s["g_lo"], 1)

            def c(j, r, turn):
                y = psY[r % 2][:].rearrange("p (h a d) -> p h a d", h=BH, a=2)
                for half in range(BH):
                    if half == 0:
                        wait(dve, "yhi", j * BH + BH)
                    v.scalar_tensor_tensor(YS[r][:, half, :], y[:, half, 1, :], Ids[r][:, half, 1:2].bitcast(F32),
                                           YS[r][:, half, :], ALU.mult, ALU.add).then_inc(s[f"ys{r % 2}"], 1)

            run_blocks(dve, block_pipeline(a, b, c))
            dve.wait_ge(s["gb_row"], B)
            for n, b in enumerate(DVE_OUT):
                result(dve, v, b, n, ("ysum", "ygb", "yfin"))

        @block.tensor
        def _(pe):
            mm = nc.tensor.matmul
            pe.wait_ge(s["wmod_in"], 16)
            pe.wait_ge(s["silu_dve"], 2)
            for j in range(2):
                ins = mm(psT[:, j * B:(j + 1) * B], Wmod[:, j * D:(j + 1) * D], SilC[:], start=True, stop=True)
            ins.then_inc(s["cols_ps"], 1)
            pe.wait_ge(s["ident"], 1)
            pe.wait_ge(s["cols"], 2)

            def transpose(b, u):
                wait(pe, "xhat1", C * b + C)
                wait(pe, "rows", b)
                for c in range(C):
                    ins = nc.tensor.transpose(psT[:, c * P:(c + 1) * P], Xh[:, c, :], Id[:])
                ins.then_inc(s["xT1"], 1)

            def query(b, u):
                pe.wait_ge(s["proj_in"], 96)
                wait(pe, "hT", b + 1)
                wait(pe, "vg", C * b)
                mm(pjA[0:LR, :], W1k[:], HT[:], start=True, stop=True).then_inc(s["uT_ps"], 1)

            def query_q(b, u):
                mm(pjB[:], Wq[:], HT[:], start=True, stop=True).then_inc(s["q_ps"], 1)

            def gates(b, u):
                wait(pe, "uT", b + 1)
                mm(pjA[:], W2k[:], UT[:], start=True, stop=True).then_inc(s["gl_ps"], 1)

            def gates_k(b, u):
                wait(pe, "q_sb", b + 1)
                mm(pjB[:], Wk[:], HT[:], start=True, stop=True).then_inc(s["k_ps"], 1)

            def values(b, u, c):
                if c == 0:
                    wait(pe, "gl_sb", b + 1)
                elif c == 1:
                    wait(pe, "k_sb", b + 1)
                else:
                    wait(pe, "vg", C * b + c - 1)
                mm((pjA, pjB)[c % 2][:], HT[:, c * P:(c + 1) * P], Wvg[:], start=True, stop=True).then_inc(s["vg_ps"], 1)

            def score(b, u, c):
                if c >= 2:
                    wait(pe, "pt", C * b + c - 1)
                else:
                    wait(pe, "qblk", H * b + H)
                    wait(pe, "oT", 2 * b)
                ps = (psS0, psS1)[c % 2][:].rearrange("p (h i t) -> p h i t", h=H, i=NS)
                for i in range(NS):
                    t0 = c * P + i * SUB
                    ins = mm(ps[:, :, i, :], KT[:, c, i, :], QB[:, :, t0:t0 + SUB], start=True, stop=True)
                ins.then_inc(s["sc_ps"], 1)

            def chunk(b, u, c):
                if c == 0:
                    wait(pe, "qs", b + 1)
                    wait(pe, "at_g", b)
                if c == 2:
                    wait(pe, "o_sb", 2 * b + 1)
                o = psO[:, (c % 2) * DV:(c % 2 + 1) * DV]
                wait(pe, "pt", C * b + c + 1)
                if c:
                    wait(pe, "s_st", 3 * b + c)
                    mm(o, QS[:, c * P:(c + 1) * P], S[c - 1][:], start=True, stop=False, skip_group_check=True)
                for h in range(H):
                    ins = mm(o[:, h * HV:(h + 1) * HV], PT[c % 2][:, h, :], VG[:, c, h * HV:(h + 1) * HV],
                             start=(c == 0), stop=(c == 0 or h == H - 1), skip_group_check=True)
                ins.then_inc(s["o_ps"], 1)

            def scores(b, u):
                wait(pe, "ktil", (NS + 1) * b + NS + 1)
                wait(pe, "s_tmp", 2 * b)
                for c in range(3):
                    ins = nc.tensor.transpose(psK[:, c * P:(c + 1) * P], KE[:, c, :], Id[:])
                ins.then_inc(s["ket_ps"], 1)

            def modulation(b, u):
                wait(pe, "silu_b", b + 1)
                wait(pe, "slot", b - 1)
                mm(psT[:], SilB[:], Wmod[:, 2 * D:6 * D], start=True, stop=True).then_inc(s["rows_ps"], 1)

            def state(b, u):
                wait(pe, "ket", b + 1)
                wait(pe, "vg", C * b + C)
                for c in range(3):
                    ds = psD[:, c * DV:(c + 1) * DV] if c < 2 else psK[:, 0:DV]
                    ins = mm(ds, KEt[:, c, :], VG[:, c, 0:DV], start=True, stop=True)
                ins.then_inc(s["ds_ps"], 1)

            def output_transpose(b, u):
                wait(pe, "onrm", b + 1)
                wait(pe, "pt", C * b + C)
                for j, ps in enumerate((psS0, psS1)):
                    for c in range(C):
                        ins = nc.tensor.transpose(ps[:, c * P:(c + 1) * P], O[:, c, j * P:(j + 1) * P], Id[:])
                    ins.then_inc(s["oT_ps"], 1)

            def project(b, u):
                wait(pe, "wo_fin", 1)
                wait(pe, "oT", 2 * b + 2)
                wait(pe, "o_sb", 2 * b + 2)
                for c in range(C):
                    for j in range(2):
                        ins = mm(psO[:, c * P:(c + 1) * P], OT[:, j, c * P:(c + 1) * P], Wo[:, j, :],
                                 start=(j == 0), stop=(j == 1))
                ins.then_inc(s["at_ps"], 1)

            def logits(b, u):
                wait(pe, "h2", 2 * b + 2)
                if not isinstance(b, int) or b < B - 2:
                    wait(pe, "hT", b + 3)
                wait(pe, "rows", b + 2 if not isinstance(b, int) or b < B - 1 else B)
                for c in range(C):
                    ins = nc.tensor.transpose(psT[:, c * P:(c + 1) * P], H2[:, c, :], Id[:])
                ins.then_inc(s["xT2"], 1)

            def logits_mm(b, u):
                wait(pe, "h2T", b + 1)
                wait(pe, "attn_in", 64)
                for c in range(C):
                    ins = mm(psT[:, c * E:(c + 1) * E], H2T[:, c * P:(c + 1) * P], Rw[:], start=True, stop=True)
                ins.then_inc(s["lg_ps"], 1)

            def rank(b, u):
                wait(pe, "lg", b + 1)
                wait(pe, "count", b * C + C)
                pos = psT[:, 2 * C * E:3 * C * E]
                mm(pos, Earlier[:], Sel[:].rearrange("p c e -> p (c e)"), start=True, stop=False)
                mm(pos, Ones[:], Count[:, 0:C, :].rearrange("p c e -> p (c e)"), start=False, stop=True).then_inc(s["pos_ps"], 1)

            pipeline(pe, (
                "p1_transpose+1 p2_chunk1+0 p1_rank+1 p1_query+1 p1_gates+1 p1_keys+1 p2_score2+0 "
                "p2_score3+0 p2_chunk2+0 p2_chunk3+0 p3_transpose-1 p1_values0+1 p1_values1+1 "
                "p1_values2+1 p1_values3+1 p3_logits-1 p2_transpose+0 p2_project+0 p2_keysT+1 p3_rank-1 "
                "p2_score0+1 p2_score1+1 p2_rows+1 p2_state+1 p2_chunk0+1"),
                     p1_transpose=transpose, p1_rank=query, p1_query=query_q, p1_gates=gates, p1_keys=gates_k,
                     p1_values0=part(values, 0), p1_values1=part(values, 1), p1_values2=part(values, 2),
                     p1_values3=part(values, 3), p2_keysT=scores, p2_score0=part(score, 0), p2_score1=part(score, 1),
                     p2_rows=modulation, p2_state=state, p2_chunk0=part(chunk, 0), p2_chunk1=part(chunk, 1),
                     p2_score2=part(score, 2), p2_score3=part(score, 3), p2_chunk2=part(chunk, 2),
                     p2_chunk3=part(chunk, 3), p2_transpose=output_transpose, p2_project=project,
                     p3_transpose=logits, p3_logits=logits_mm, p3_rank=rank)

            pe.wait_ge(s["slot"], B)
            mm(psT[:, 0:E], Ones[:], Count[:, C, :], start=True, stop=True).then_inc(s["cnt_ps"], 1)
            pe.wait_ge(s["tab_e"], 1)
            pe.wait_ge(s["w_lo"], TOP * E)
            pe.wait_ge(s["at_g"], B)

            def expert(j):
                at = Tab[0:1, 1, j:j + 1] if isinstance(j, int) else Tab[0:1, 1, bass.ds(j, 1)]
                return pe.value_load(at, min_val=0, max_val=E - 1)

            def a(j, r, turn):
                wait(pe, f"xblk{r}", turn * 16 + 16)
                wait(pe, "xt_lo", j - 1)
                for half in range(BH):
                    ins = nc.tensor.transpose(psX[r % 2][:, half * P:(half + 1) * P], XR[r][:, half, 0:D], Id[:])
                ins.then_inc(s["xt_ps"], 1)

            def b(j, r, turn):
                wait(pe, "xt_lo", j + 1)
                wait(pe, "w1_b", j + 1)
                wait(pe, "gelu", (j - 1) * HB)
                for n in range(HB):
                    for i in range(KB):
                        k = n * KB + i
                        o = psH[r % 2][n][:, i * BT:(i + 1) * BT]
                        w1 = [W1b[r % 2][:, part, k * P:(k + 1) * P] for part in range(2)]
                        mm(o, w1[0], XThi[r % 2][:], start=True, stop=False)
                        mm(o, w1[0], XTlo[r % 2][:], start=False, stop=False)
                        ins = mm(o, w1[1], XThi[r % 2][:], start=False, stop=True)
                    ins.then_inc(s["h_ps"], 1)

            def c(j, r, turn):
                e = expert(j)
                wait(pe, f"ys{r % 2}", turn * (BH * RING // 2) + r // 2 * BH)
                wait(pe, "g_lo", j * HB + HB)
                for half in range(BH):
                    t = slice(half * P, (half + 1) * P)
                    o = psY[r % 2][:, half * 2 * D:(half + 1) * 2 * D]
                    for k in range(KH):
                        w2 = W2[:, bass.ds(e, 1), k, :, :].rearrange("p o a d -> p (o a d)")
                        mm(o, Ghi[r % 2][:, k, t], w2, start=(k == 0), stop=False, skip_group_check=True)
                        ins = mm(o[:, 0:D], Glo[r % 2][:, k, t], w2[:, 0:D], start=False, stop=(k == KH - 1),
                                 skip_group_check=True)
                ins.then_inc(s["y_ps"], 1)

            run_blocks(pe, block_pipeline(a, b, c))


_INS = ["x", "cT", "wmod", "wq", "wk", "wvg", "gk_w1", "gk_w2", "gk_b", "wo", "rms_w", "rwT", "w1T", "w2T"]


def kernel(**inputs):
    import concourse.bacc as bacc
    from concourse.bass_utils import run_bass_kernel_spmd

    i = {k.removeprefix("L0_"): np.asarray(v) for k, v in inputs.items()}
    laid = {
        "x": i["attn_x"],
        "cT": i["c"].T,
        "wmod": i["wmod"],
        "wq": i["attn_Wq"],
        "wk": i["attn_Wk"],
        "wvg": np.concatenate([i["attn_Wv"], i["attn_Wg"]], axis=1),
        "gk_w1": i["attn_gk_w1"],
        "gk_w2": i["attn_gk_w2"],
        "gk_b": i["attn_gk_b"].reshape(DK, 1),
        "wo": i["attn_Wo"].reshape(2, P, D).transpose(1, 0, 2),
        "rms_w": i["attn_rms_w"].reshape(HV, 1),
        "rwT": i["ffn_router_w"].T,
        "w1T": i["ffn_w1"].transpose(2, 0, 1),
        "w2T": i["ffn_w2"].reshape(E, D, KH, P).transpose(3, 0, 2, 1).reshape(P, E, HID),
    }
    nc = bacc.Bacc("TRN2", target_bir_lowering=False, num_devices=1)
    arrays, args = {}, []
    for name in _INS:
        a = np.ascontiguousarray(laid[name])
        arrays[f"in_{name}"] = a
        args.append(nc.dram_tensor(f"in_{name}", a.shape, mybir.dt.from_np(a.dtype), kind="ExternalInput").ap())
    args.append(nc.dram_tensor("out", (B, T, D), F32, kind="ExternalOutput").ap())
    build_program(nc, *args)
    r = run_bass_kernel_spmd(nc, [arrays], core_ids=[0])
    return r.results[0]["out"]
```
